# Optimizing a Trainium2 kernel written in Bass

```python
import numpy as np
import jax
import jax.numpy as jnp

def _softmax(x, axis=-1):
    return jax.nn.softmax(x, axis=axis)

def _gelu(x):
    return jax.nn.gelu(x, approximate=True)

def _silu(x):
    return jax.nn.silu(x)

def _sigmoid(x):
    return jax.nn.sigmoid(x)

def _layernorm(x, axis=-1, eps=1e-05):
    m = jnp.mean(x, axis=axis, keepdims=True)
    v = jnp.var(x, axis=axis, keepdims=True)
    return (x - m) / jnp.sqrt(v + eps)

def _scatter_add(tgt, idx, src, axis=0):
    return tgt.at[idx].add(src)

def _segment_sum(src, seg, n):
    return jax.ops.segment_sum(src, seg, n)
kernel_name = 'mk_prb_d1_jaxref_r8_40f429'

def setup_inputs(seed: int=0):
    np.random.seed(seed)
    _w = jnp.asarray

    def _L0_attn_setup():
        import jax, jax.numpy as jnp
        import numpy as np
        D_MODEL = 128
        NUM_HEADS = 16
        HEAD_DIM = D_MODEL // NUM_HEADS
        WINDOW = 16
        DILATION = 3
        SCALE = HEAD_DIM ** (-0.5)

        def _linear(x, W, b):
            return x @ W.T + b

        def _chunk_attention(x, Wq, bq, Wk, bk, Wv, bv, chunk):
            B, L, D = x.shape
            pad = -L % chunk
            if pad:
                x = jnp.pad(x, ((0, 0), (0, pad), (0, 0)))
            Lp = L + pad
            nC = Lp // chunk
            xr = x.reshape(B * nC, chunk, D)

            def heads(t):
                return t.reshape(B * nC, chunk, NUM_HEADS, HEAD_DIM).transpose(0, 2, 1, 3)
            q = heads(_linear(xr, Wq, bq))
            k = heads(_linear(xr, Wk, bk))
            v = heads(_linear(xr, Wv, bv))
            attn = jax.nn.softmax(jnp.einsum('bhqd,bhkd->bhqk', q, k) * SCALE, axis=-1)
            out = jnp.einsum('bhqk,bhkd->bhqd', attn, v)
            out = out.transpose(0, 2, 1, 3).reshape(B, Lp, D)
            return out[:, :L, :]
        key = jax.random.key(seed)
        ks = jax.random.split(key, 9)
        s = 1.0 / np.sqrt(D_MODEL)
        x = jax.random.normal(ks[0], (4, 512, D_MODEL), dtype=jnp.float32)

        def lin(kw, kb):
            W = jax.random.uniform(kw, (D_MODEL, D_MODEL), minval=-s, maxval=s, dtype=jnp.float32)
            b = jax.random.uniform(kb, (D_MODEL,), minval=-s, maxval=s, dtype=jnp.float32)
            return (W, b)
        Wq, bq = lin(ks[1], ks[2])
        Wk, bk = lin(ks[3], ks[4])
        Wv, bv = lin(ks[5], ks[6])
        Wo, bo = lin(ks[7], ks[8])
        return {'x': x, 'Wq': Wq, 'bq': bq, 'Wk': Wk, 'bk': bk, 'Wv': Wv, 'bv': bv, 'Wo': Wo, 'bo': bo}
    _L0_attn_in = _L0_attn_setup()

    def _L0_ffn_setup():
        import jax, jax.numpy as jnp
        import numpy as np
        H = 128
        NH = 16
        HD = H // NH
        HH = HD // 2
        L = H // 4
        I = int(H * 1.0)
        ER = 7
        TOPK = 2
        BASE = 10000.0
        EPS = 1e-05

        def rmsnorm(x, w):
            norm = jnp.sqrt(jnp.mean(x * x, axis=-1, keepdims=True)) + EPS
            return x / norm * w

        def rope_tables(seq_len):
            inv_freq = 1.0 / BASE ** (jnp.arange(0, HH, 2, dtype=jnp.float32) / HH)
            t = jnp.arange(seq_len, dtype=jnp.float32)
            freqs = jnp.einsum('i,j->ij', t, inv_freq)
            emb = jnp.concatenate([freqs, freqs], axis=-1)
            cos = jnp.cos(emb)[None, :, None, :]
            sin = jnp.sin(emb)[None, :, None, :]
            return (cos, sin)

        def rotate_half(x):
            x1, x2 = jnp.split(x, 2, axis=-1)
            return jnp.concatenate([-x2, x1], axis=-1)

        def silu(x):
            return x * jax.nn.sigmoid(x)

        def mla(xn, W_kvd, W_qd, W_ku, W_qu, W_vu, W_ropeq, W_ropek, W_o):
            B, S, _ = xn.shape
            kv_lat = xn @ W_kvd
            q_lat = xn @ W_qd
            k = (kv_lat @ W_ku).reshape(B, S, NH, HH)
            q = (q_lat @ W_qu).reshape(B, S, NH, HH)
            v = (kv_lat @ W_vu).reshape(B, S, NH, HD)
            q_rope = (q_lat @ W_ropeq).reshape(B, S, NH, HH)
            k_rope = (xn @ W_ropek).reshape(B, S, NH, HH)
            cos, sin = rope_tables(S)
            k_rope = k_rope * cos + rotate_half(k_rope) * sin
            q_rope = q_rope * cos + rotate_half(q_rope) * sin
            kk = jnp.concatenate([k, k_rope], axis=-1)
            qq = jnp.concatenate([q, q_rope], axis=-1)
            scale = 1.0 / jnp.sqrt(jnp.float32(HD))
            scores = jnp.einsum('bqhd,bkhd->bhqk', qq, kk) * scale
            causal = jnp.tril(jnp.ones((S, S), dtype=bool))
            scores = jnp.where(causal[None, None], scores, jnp.finfo(scores.dtype).min)
            probs = jax.nn.softmax(scores, axis=-1)
            y = jnp.einsum('bhqk,bkhd->bqhd', probs, v).reshape(B, S, H)
            return y @ W_o

        def moe(xn, Wg_s, Wu_s, Wd_s, Wg_r, Wu_r, Wd_r, W_router, routing_bias):
            B, S, _ = xn.shape
            xt = xn.reshape(B * S, H)
            shared = silu(xt @ Wg_s) * (xt @ Wu_s) @ Wd_s
            logits = xt @ W_router + routing_bias
            probs = jax.nn.sigmoid(logits)
            scores, idx = jax.lax.top_k(probs, TOPK)
            scores = scores / jnp.sum(scores, axis=-1, keepdims=True)
            wts = jnp.sum(jax.nn.one_hot(idx, ER, dtype=xt.dtype) * scores[..., None], axis=1)
            g = jnp.einsum('th,ehi->tei', xt, Wg_r)
            u = jnp.einsum('th,ehi->tei', xt, Wu_r)
            hmid = silu(g) * u
            combined = jnp.einsum('tei,eih,te->th', hmid, Wd_r, wts)
            return (shared + combined).reshape(B, S, H)
        key = jax.random.key(seed)
        ks = jax.random.split(key, 20)
        s = 0.02
        r = lambda k, shp: jax.random.normal(k, shp, dtype=jnp.float32) * s
        return {'x': jax.random.normal(ks[0], (4, 128, H), dtype=jnp.float32), 'w_ln1': jnp.ones((H,), jnp.float32), 'w_ln2': jnp.ones((H,), jnp.float32), 'W_kvd': r(ks[1], (H, L)), 'W_qd': r(ks[2], (H, L)), 'W_ku': r(ks[3], (L, NH * HH)), 'W_qu': r(ks[4], (L, NH * HH)), 'W_vu': r(ks[5], (L, H)), 'W_ropeq': r(ks[6], (L, H // 2)), 'W_ropek': r(ks[7], (H, H // 2)), 'W_o': r(ks[8], (H, H)), 'Wg_s': r(ks[9], (H, I)), 'Wu_s': r(ks[10], (H, I)), 'Wd_s': r(ks[11], (I, H)), 'Wg_r': r(ks[12], (ER, H, I)), 'Wu_r': r(ks[13], (ER, H, I)), 'Wd_r': r(ks[14], (ER, I, H)), 'W_router': r(ks[15], (H, ER)), 'routing_bias': jnp.zeros((ER,), jnp.float32)}
    _L0_ffn_in = _L0_ffn_setup()
    _d = {'L0_attn_x': _L0_attn_in['x'], 'L0_attn_Wq': _L0_attn_in['Wq'], 'L0_attn_bq': _L0_attn_in['bq'], 'L0_attn_Wk': _L0_attn_in['Wk'], 'L0_attn_bk': _L0_attn_in['bk'], 'L0_attn_Wv': _L0_attn_in['Wv'], 'L0_attn_bv': _L0_attn_in['bv'], 'L0_attn_Wo': _L0_attn_in['Wo'], 'L0_attn_bo': _L0_attn_in['bo'], 'L0_ffn_w_ln1': _L0_ffn_in['w_ln1'], 'L0_ffn_w_ln2': _L0_ffn_in['w_ln2'], 'L0_ffn_W_kvd': _L0_ffn_in['W_kvd'], 'L0_ffn_W_qd': _L0_ffn_in['W_qd'], 'L0_ffn_W_ku': _L0_ffn_in['W_ku'], 'L0_ffn_W_qu': _L0_ffn_in['W_qu'], 'L0_ffn_W_vu': _L0_ffn_in['W_vu'], 'L0_ffn_W_ropeq': _L0_ffn_in['W_ropeq'], 'L0_ffn_W_ropek': _L0_ffn_in['W_ropek'], 'L0_ffn_W_o': _L0_ffn_in['W_o'], 'L0_ffn_Wg_s': _L0_ffn_in['Wg_s'], 'L0_ffn_Wu_s': _L0_ffn_in['Wu_s'], 'L0_ffn_Wd_s': _L0_ffn_in['Wd_s'], 'L0_ffn_Wg_r': _L0_ffn_in['Wg_r'], 'L0_ffn_Wu_r': _L0_ffn_in['Wu_r'], 'L0_ffn_Wd_r': _L0_ffn_in['Wd_r'], 'L0_ffn_W_router': _L0_ffn_in['W_router'], 'L0_ffn_routing_bias': _L0_ffn_in['routing_bias']}
    _x0 = _d['L0_attn_x']
    _d['L0_attn_x'] = jax.random.normal(jax.random.fold_in(jax.random.key(seed), 1), (4, 512, 128), dtype=_x0.dtype)
    del _x0
    return _d

def reference(L0_attn_x, L0_attn_Wq, L0_attn_bq, L0_attn_Wk, L0_attn_bk, L0_attn_Wv, L0_attn_bv, L0_attn_Wo, L0_attn_bo, L0_ffn_w_ln1, L0_ffn_w_ln2, L0_ffn_W_kvd, L0_ffn_W_qd, L0_ffn_W_ku, L0_ffn_W_qu, L0_ffn_W_vu, L0_ffn_W_ropeq, L0_ffn_W_ropek, L0_ffn_W_o, L0_ffn_Wg_s, L0_ffn_Wu_s, L0_ffn_Wd_s, L0_ffn_Wg_r, L0_ffn_Wu_r, L0_ffn_Wd_r, L0_ffn_W_router, L0_ffn_routing_bias):

    def _L0_attn_ref(x, Wq, bq, Wk, bk, Wv, bv, Wo, bo):
        import jax, jax.numpy as jnp
        import numpy as np
        D_MODEL = 128
        NUM_HEADS = 16
        HEAD_DIM = D_MODEL // NUM_HEADS
        WINDOW = 16
        DILATION = 3
        SCALE = HEAD_DIM ** (-0.5)

        def _linear(x, W, b):
            return x @ W.T + b

        def _chunk_attention(x, Wq, bq, Wk, bk, Wv, bv, chunk):
            B, L, D = x.shape
            pad = -L % chunk
            if pad:
                x = jnp.pad(x, ((0, 0), (0, pad), (0, 0)))
            Lp = L + pad
            nC = Lp // chunk
            xr = x.reshape(B * nC, chunk, D)

            def heads(t):
                return t.reshape(B * nC, chunk, NUM_HEADS, HEAD_DIM).transpose(0, 2, 1, 3)
            q = heads(_linear(xr, Wq, bq))
            k = heads(_linear(xr, Wk, bk))
            v = heads(_linear(xr, Wv, bv))
            attn = jax.nn.softmax(jnp.einsum('bhqd,bhkd->bhqk', q, k) * SCALE, axis=-1)
            out = jnp.einsum('bhqk,bhkd->bhqd', attn, v)
            out = out.transpose(0, 2, 1, 3).reshape(B, Lp, D)
            return out[:, :L, :]
        B, L, D = x.shape
        local_out = _chunk_attention(x, Wq, bq, Wk, bk, Wv, bv, WINDOW)
        pad = -L % DILATION
        x_pad = jnp.pad(x, ((0, 0), (0, pad), (0, 0))) if pad else x
        Lp = L + pad
        xv = x_pad.reshape(B, Lp // DILATION, DILATION, D).transpose(0, 2, 1, 3)
        x_atrous = xv.reshape(B * DILATION, Lp // DILATION, D)
        a = _chunk_attention(x_atrous, Wq, bq, Wk, bk, Wv, bv, WINDOW)
        a = a.reshape(B, DILATION, Lp // DILATION, D).transpose(0, 2, 1, 3).reshape(B, Lp, D)
        atrous_out = a[:, :L, :]
        return _linear(local_out + atrous_out, Wo, bo)

    def _L0_ffn_ref(x, w_ln1, w_ln2, W_kvd, W_qd, W_ku, W_qu, W_vu, W_ropeq, W_ropek, W_o, Wg_s, Wu_s, Wd_s, Wg_r, Wu_r, Wd_r, W_router, routing_bias):
        import jax, jax.numpy as jnp
        import numpy as np
        H = 128
        NH = 16
        HD = H // NH
        HH = HD // 2
        L = H // 4
        I = int(H * 1.0)
        ER = 7
        TOPK = 2
        BASE = 10000.0
        EPS = 1e-05

        def rmsnorm(x, w):
            norm = jnp.sqrt(jnp.mean(x * x, axis=-1, keepdims=True)) + EPS
            return x / norm * w

        def rope_tables(seq_len):
            inv_freq = 1.0 / BASE ** (jnp.arange(0, HH, 2, dtype=jnp.float32) / HH)
            t = jnp.arange(seq_len, dtype=jnp.float32)
            freqs = jnp.einsum('i,j->ij', t, inv_freq)
            emb = jnp.concatenate([freqs, freqs], axis=-1)
            cos = jnp.cos(emb)[None, :, None, :]
            sin = jnp.sin(emb)[None, :, None, :]
            return (cos, sin)

        def rotate_half(x):
            x1, x2 = jnp.split(x, 2, axis=-1)
            return jnp.concatenate([-x2, x1], axis=-1)

        def silu(x):
            return x * jax.nn.sigmoid(x)

        def mla(xn, W_kvd, W_qd, W_ku, W_qu, W_vu, W_ropeq, W_ropek, W_o):
            B, S, _ = xn.shape
            kv_lat = xn @ W_kvd
            q_lat = xn @ W_qd
            k = (kv_lat @ W_ku).reshape(B, S, NH, HH)
            q = (q_lat @ W_qu).reshape(B, S, NH, HH)
            v = (kv_lat @ W_vu).reshape(B, S, NH, HD)
            q_rope = (q_lat @ W_ropeq).reshape(B, S, NH, HH)
            k_rope = (xn @ W_ropek).reshape(B, S, NH, HH)
            cos, sin = rope_tables(S)
            k_rope = k_rope * cos + rotate_half(k_rope) * sin
            q_rope = q_rope * cos + rotate_half(q_rope) * sin
            kk = jnp.concatenate([k, k_rope], axis=-1)
            qq = jnp.concatenate([q, q_rope], axis=-1)
            scale = 1.0 / jnp.sqrt(jnp.float32(HD))
            scores = jnp.einsum('bqhd,bkhd->bhqk', qq, kk) * scale
            causal = jnp.tril(jnp.ones((S, S), dtype=bool))
            scores = jnp.where(causal[None, None], scores, jnp.finfo(scores.dtype).min)
            probs = jax.nn.softmax(scores, axis=-1)
            y = jnp.einsum('bhqk,bkhd->bqhd', probs, v).reshape(B, S, H)
            return y @ W_o

        def moe(xn, Wg_s, Wu_s, Wd_s, Wg_r, Wu_r, Wd_r, W_router, routing_bias):
            B, S, _ = xn.shape
            xt = xn.reshape(B * S, H)
            shared = silu(xt @ Wg_s) * (xt @ Wu_s) @ Wd_s
            logits = xt @ W_router + routing_bias
            probs = jax.nn.sigmoid(logits)
            scores, idx = jax.lax.top_k(probs, TOPK)
            scores = scores / jnp.sum(scores, axis=-1, keepdims=True)
            wts = jnp.sum(jax.nn.one_hot(idx, ER, dtype=xt.dtype) * scores[..., None], axis=1)
            g = jnp.einsum('th,ehi->tei', xt, Wg_r)
            u = jnp.einsum('th,ehi->tei', xt, Wu_r)
            hmid = silu(g) * u
            combined = jnp.einsum('tei,eih,te->th', hmid, Wd_r, wts)
            return (shared + combined).reshape(B, S, H)
        x = x + mla(rmsnorm(x, w_ln1), W_kvd, W_qd, W_ku, W_qu, W_vu, W_ropeq, W_ropek, W_o)
        x = x + moe(rmsnorm(x, w_ln2), Wg_s, Wu_s, Wd_s, Wg_r, Wu_r, Wd_r, W_router, routing_bias)
        return x
    x = L0_attn_x
    xn = _layernorm(x, axis=-1)
    x = x + _L0_attn_ref(xn, L0_attn_Wq, L0_attn_bq, L0_attn_Wk, L0_attn_bk, L0_attn_Wv, L0_attn_bv, L0_attn_Wo, L0_attn_bo) + _L0_ffn_ref(xn, L0_ffn_w_ln1, L0_ffn_w_ln2, L0_ffn_W_kvd, L0_ffn_W_qd, L0_ffn_W_ku, L0_ffn_W_qu, L0_ffn_W_vu, L0_ffn_W_ropeq, L0_ffn_W_ropek, L0_ffn_W_o, L0_ffn_Wg_s, L0_ffn_Wu_s, L0_ffn_Wd_s, L0_ffn_Wg_r, L0_ffn_Wu_r, L0_ffn_Wd_r, L0_ffn_W_router, L0_ffn_routing_bias)
    return x

_drawn_inputs = setup_inputs


def setup_inputs(seed=0):
    import zlib

    import numpy as np

    out = dict(_drawn_inputs(seed))
    spreads = {'L0_ffn_w_ln1': (1.0, 0.6), 'L0_ffn_w_ln2': (1.0, 0.6), 'L0_ffn_routing_bias': (0.0, 0.8)}
    factors = {'L0_attn_bq': 64.0,
     'L0_attn_bk': 64.0,
     'L0_ffn_W_kvd': 8.0,
     'L0_ffn_W_qd': 8.0,
     'L0_ffn_W_ku': 8.0,
     'L0_ffn_W_qu': 8.0,
     'L0_ffn_W_vu': 8.0,
     'L0_ffn_W_ropeq': 8.0,
     'L0_ffn_W_ropek': 8.0,
     'L0_ffn_W_o': 8.0,
     'L0_ffn_Wg_s': 8.0,
     'L0_ffn_Wu_s': 8.0,
     'L0_ffn_Wd_s': 8.0,
     'L0_ffn_Wg_r': 8.0,
     'L0_ffn_Wu_r': 8.0,
     'L0_ffn_Wd_r': 8.0,
     'L0_ffn_W_router': 8.0,
     'L0_attn_Wq': 8.0,
     'L0_attn_Wk': 8.0,
     'L0_attn_Wv': 5.499,
     'L0_attn_bv': 8.0,
     'L0_attn_Wo': 4.961,
     'L0_attn_bo': 8.0}
    for name, (base, spread) in spreads.items():
        noise = np.random.default_rng([zlib.crc32(name.encode()), seed]).standard_normal(out[name].shape)
        drawn = base * np.exp(spread * noise) if base else spread * noise
        out[name] = jnp.asarray(drawn.astype(out[name].dtype))
    for name, factor in factors.items():
        out[name] = (out[name] * factor).astype(out[name].dtype)
    return out
```

```python
from contextlib import ExitStack

import numpy as np

import concourse.bass as bass
from concourse import mybir

F32 = mybir.dt.float32
BF16 = mybir.dt.bfloat16
U32 = mybir.dt.uint32
ALU = mybir.AluOpType
ACT = mybir.ActivationFunctionType
AX = mybir.AxisListType

P = 128
B = 4
S = 512
D = 128
H = 16
HD = 8
HH = HD // 2
LAT = D // 4
NT = S // P
TILES = B * NT
CHUNK = 16
DIL = 3
PAIR = 2 * CHUNK
LPH = -(-S // DIL)
LPH_PAIRS = -(-LPH // PAIR)
SX = LPH_PAIRS * PAIR * DIL
ER = 7
NE = ER + 1
LN_EPS = 1e-5
RMS_EPS = 1e-5
SCALE = float(HD) ** -0.5
NEG = -1e30
TERMS = 6
Q_PARTS = (0, 0, 1, 0, 2, 1)
K_PARTS = (0, 1, 0, 2, 0, 1)
SLOT = 64
SHIFT_ROW = TERMS * HD
P_RING = 2

GROUPS = [[("local", g * PAIR, 1) for g in range(S // PAIR)],
          [("dilated", r + DIL * PAIR * g, DIL) for r in range(DIL) for g in range(LPH_PAIRS)]]
LTILES = [gs[n:n + 4] for gs in GROUPS for n in range(0, len(gs), 4)]
NLT = len(LTILES)


def score_units():
    units = []
    for i in range(NT):
        n = S // ((i + 1) * P)
        units += [(i, list(range(h, min(h + n, H)))) for h in range(0, H, n)]
    return units


UNITS = score_units()


def merged(*lists):
    keyed = [((k + 0.5) / len(one), n, k, step) for n, one in enumerate(lists) for k, step in enumerate(one)]
    return [x[3] for x in sorted(keyed, key=lambda x: x[:3])]


def plan():
    def projections(b):
        return [("XT", b, 0), ("XT", b, 1), ("LQ", b), ("LK", b), ("MA", b, 0), ("MB", b, 0), ("MA", b, 1), ("MB", b, 1), ("MV", b)]

    def maxima(b):
        return [("S", b, u) for u in range(len(UNITS))] + [("SHIFT", b)]

    def latent(b):
        steps, late = [], []
        for g in range(H // 4):
            for j in range(NT):
                steps.append(("E", b, g, j))
                if late:
                    steps.append(late.pop())
                late.append(("PV", b, g, j))
        steps += late + [("Y", b, i) for i in range(NT)] + [("YT", b), ("X1", b)]
        return steps

    def local(b):
        stages = ["LV", "LS", "LO", "LY", "LT"]
        steps = []
        for k in range(NLT + len(stages) - 1):
            for s in reversed(range(len(stages))):
                if 0 <= k - s < NLT:
                    steps.append((stages[s], b, k - s))
        return steps + [("LW", b)]

    steps = [("WF",)] + projections(0) + [("KD", 0)] + maxima(0)
    for b in range(B):
        if b + 1 < B:
            steps += projections(b + 1)
            steps += merged(latent(b), maxima(b + 1), local(b)) + [("KD", b + 1)]
        else:
            steps += merged(latent(b), local(b))
    steps += [("X2T", b) for b in range(B)] + [("ROUTE",)]
    moe = [(c, e) for c in range(B) for e in range(NE)]
    for n in range(len(moe) + 2):
        if n < len(moe):
            steps.append(("GU",) + moe[n])
        if n >= 1 and n - 1 < len(moe):
            steps.append(("DOWN",) + moe[n - 1])
        if n >= 2:
            steps.append(("ADD",) + moe[n - 2])
    return steps


MISC = {"WF", "XT", "LQ", "LK", "MA", "MB", "MV", "SHIFT", "Y", "YT", "X1", "LV", "LO", "LY", "LT", "LW", "X2T", "ROUTE"}


def numbers(steps, kinds):
    return {s: n + 1 for n, s in enumerate([s for s in steps if s[0] in kinds])}


def as_bf16(a):
    bits = np.ascontiguousarray(a, np.float32).view(np.uint32).astype(np.uint64)
    return ((bits + 0x7FFF + ((bits >> 16) & 1)) >> 16).astype(np.uint16)


def constants():
    eye = np.eye(P, dtype=np.float32)
    q, k = np.arange(P)[:, None], np.arange(P)[None, :]
    causal = np.where(k > q, NEG, 0.0).astype(np.float32)
    row_chunk = (np.arange(P)[:, None] // CHUNK) % 2
    col_chunk = (np.arange(H * PAIR)[None, :] // CHUNK) % 2
    pair = np.where(row_chunk != col_chunk, NEG, 0.0).astype(np.float32)
    inv = 1.0 / np.float32(10000.0) ** (np.arange(0, HH, 2, dtype=np.float32) / np.float32(HH))
    freqs = np.outer(np.arange(S, dtype=np.float32), inv.astype(np.float32))
    emb = np.concatenate([freqs, freqs], axis=-1)
    cos, sin = np.cos(emb).astype(np.float32), np.sin(emb).astype(np.float32)
    sin[:, :HH // 2] *= -1
    cosT = np.concatenate([np.ones((HH, S), np.float32), cos.T])
    sinT = np.concatenate([np.zeros((HH, S), np.float32), sin.T])
    return {
        "c_eye": eye,
        "c_masks": as_bf16(np.concatenate([eye, causal, causal.T, pair], axis=1)),
        "c_rope": np.stack([np.tile(cosT, (H, 1)), np.tile(sinT, (H, 1))], axis=1),
        "c_rows": as_bf16(np.stack([np.ones(H // 2 * S, np.float32), np.zeros(H // 2 * S, np.float32)])),
        "c_experts": np.broadcast_to(np.arange(8, dtype=np.float32), (P, 8)).copy(),
    }


def build(nc, io, out):
    steps = plan()
    misc_no = numbers(steps, MISC)
    a_no = numbers(steps, {"S", "LS", "DOWN"})
    ls_no = numbers(steps, {"LS"})
    lo_no = numbers(steps, {"LO"})
    e_no = numbers(steps, {"E"})
    pv_no = numbers(steps, {"PV"})
    gu_no = numbers(steps, {"GU"})
    add_no = numbers(steps, {"ADD"})

    with ExitStack() as ctx:
        def sb(name, shape, dt=F32):
            return ctx.enter_context(nc.sbuf_tensor(name, shape, dt))

        def psum(name, shape):
            return ctx.enter_context(nc.psum_tensor(name, shape, F32))

        def sem(name):
            return ctx.enter_context(nc.semaphore(name))

        bank_a = [psum(f"bank_a{i}", [P, 512]) for i in range(2)]
        bank_b = [psum(f"bank_b{i}", [P, 2, 512]) for i in range(2)]
        bank_c = psum("bank_c", [P, 512])
        misc = psum("misc", [P, 512])

        eye = sb("eye", [P, P])
        masks = sb("masks", [P, 3 * P + 512], BF16)
        eye16, causal16, causalT16, pair16 = (masks[:, 0:P], masks[:, P:2 * P], masks[:, 2 * P:3 * P], masks[:, 3 * P:])
        rope = sb("rope", [P, 2, S])
        expert_ids = sb("expert_ids", [P, 8])
        w_attn = sb("w_attn", [P, 4, D])
        w_down_lat = sb("w_down_lat", [LAT, 2, D])
        w_up_lat = sb("w_up_lat", [LAT, 3 * 64 + D])
        w_ropek = sb("w_ropek", [P, H, HH])
        w_mla = sb("w_mla", [P, 2, 2, H, HD])
        w_mla_v = sb("w_mla_v", [P, D])
        w_mla_o = sb("w_mla_o", [P, D])
        w_router = sb("w_router", [P, ER])
        router_bias = sb("router_bias", [P, ER])
        cols = sb("cols", [P, 5])
        bo_all = sb("bo_all", [P, D])
        x = sb("x", [P, TILES, D])
        xn = sb("xn", [P, TILES, D])
        x1 = sb("x1", [P, TILES, D])
        xr = x1
        xnT = sb("xnT", [P, 2, SX])
        xrT = sb("xrT", [P, B, S])
        x2T = xrT
        stats = sb("stats", [P, TILES, 6])
        mv = sb("mv", [P, TILES, 2])
        nrm = sb("nrm", [P, 4, TILES])
        qT = sb("qT", [P, 2, SX])
        kT = sb("kT", [P, SX])
        k_diag = sb("k_diag", [P, H, SX])
        v_tile = sb("v_tile", [P, 2, H, HD])
        v_loc = sb("v_loc", [P, 2, 4, H, HD + 1])
        p_loc = sb("p_loc", [P, 2, 512])
        pT_loc = sb("pT_loc", [P, 2, 512])
        row_max = sb("row_max", [P, H])
        oT_loc = sb("oT_loc", [P, 512])
        y_loc = sb("y_loc", [P, D])
        rden = sb("rden", [P, H])
        attnT = sb("attnT", [P, SX])
        rot = sb("rot", [P, 2, S])
        turned = sb("turned", [P, S])
        parts = sb("parts", [P, 2, 3, S], BF16)
        rest = sb("rest", [P, S])
        k_stack = [sb(f"k_stack{i}", [P, H // 2, S], BF16) for i in range(2)]
        q_stack = [sb(f"q_stack{i}", [P, H // 2, 2, S], BF16) for i in range(2)]
        neg_max = sb("neg_max", [P, 2, H // 2, NT])
        shift = sb("shift", [H * NT, 2, P], BF16)
        v_mla = sb("v_mla", [P, 2, NT, H, HD + 1])
        p_mla = sb("p_mla", [P, P_RING, 4, S])
        oT_mla = sb("oT_mla", [P, 4, S])
        y_mla = sb("y_mla", [P, NT, D])
        yT_mla = oT_mla[:, 0, :]
        rden_mla = sb("rden_mla", [P, H])
        gate = [p_mla[:, 0, n, :] for n in range(2)]
        hid = [p_mla[:, 1, n, :] for n in range(2)]
        late = k_diag[:].rearrange("p h n -> p (h n)")
        w_exp = late[:, 0:NE * 3 * D].rearrange("p (e n d) -> p e n d", e=NE, n=3)
        rt = late[:, NE * 3 * D:NE * 3 * D + 6 * TILES * 8].rearrange("p (n t e) -> p n t e", n=6, t=TILES)
        rt_idx = sb("rt_idx", [P, TILES, 8], U32)
        rt_sum = sb("rt_sum", [P, 2, TILES])

        parts_dram = nc.dram_tensor("parts_dram", [B, 2, 3, P, S], BF16, kind="Internal").ap()
        shift_dram = nc.dram_tensor("shift_dram", [B, 2, H * NT, P], BF16, kind="Internal").ap()
        rows_dram = io["c_rows"].bitcast(BF16)

        x_in = [sem(f"x_in{b}") for b in range(B)]
        consts_in = sem("consts_in")
        weights_in = sem("weights_in")
        experts_in = sem("experts_in")
        k_ones_in = sem("k_ones_in")
        k_diag_in = sem("k_diag_in")
        parts_out = sem("parts_out")
        stacks_in = sem("stacks_in")
        shift_out = sem("shift_out")
        shift_in = sem("shift_in")
        out_done = sem("out_done")
        zeroed = sem("zeroed")
        xn_ready = sem("xn_ready")
        sqrt_in = sem("sqrt_in")
        sqrt_out = sem("sqrt_out")
        misc_full, misc_drained = sem("misc_full"), sem("misc_drained")
        a_full, a_drained = sem("a_full"), sem("a_drained")
        b_full, b_drained = sem("b_full"), sem("b_drained")
        pv_done, c_drained = sem("pv_done"), sem("c_drained")
        v_spread = sem("v_spread")
        loc_exp = sem("loc_exp")
        loc_turned = sem("loc_turned")
        rot_ready = sem("rot_ready")
        split_ready = sem("split_ready")
        gate_ready = sem("gate_ready")
        hid_ready = sem("hid_ready")
        probs_in, probs_out = sem("probs_in"), sem("probs_out")
        xres_ready = sem("xres_ready")
        sum_ready = sem("sum_ready")
        v_step, g_step, s_step = sem("v_step"), sem("g_step"), sem("s_step")

        def tokens(first, step, n=PAIR):
            return slice(first, first + step * (n - 1) + 1, step)

        def runs(tile):
            found = []
            for n, (_, first, step) in enumerate(tile):
                if found and found[-1][2] + found[-1][1] * PAIR * step == first:
                    found[-1][1] += 1
                else:
                    found.append([n, 1, first, step])
            return found

        E_PER_B = NT * (H // 4)
        BOTH_IN = 16 * 2 * (TERMS * 2) + 16 * 4
        V_INIT = 3

        block = ctx.enter_context(nc.Block())

        @block.sync
        def _(sp):
            xv = io["x"].rearrange("b (i p) d -> p b i d", p=P)
            for b in range(B):
                sp.dma_start(x[:, b * NT:(b + 1) * NT, :], xv[:, b]).then_inc(x_in[b], 16)
            for dst, src in ((eye[:], io["c_eye"]), (masks[:], io["c_masks"].bitcast(BF16)), (rope[:], io["c_rope"]),
                             (expert_ids[:], io["c_experts"])):
                sp.dma_start(dst, src).then_inc(consts_in, 16)
            for n, name in enumerate(("Wq", "Wk", "Wv", "Wo")):
                sp.dma_start(w_attn[:, n, :], io[name]).then_inc(weights_in, 16)
            sp.dma_start(w_down_lat[:, 0, :], io["W_kvd"]).then_inc(weights_in, 16)
            sp.dma_start(w_down_lat[:, 1, :], io["W_qd"]).then_inc(weights_in, 16)
            for n, name in enumerate(("W_ku", "W_qu", "W_ropeq")):
                sp.dma_start(w_up_lat[:, 64 * n:64 * n + 64], io[name]).then_inc(weights_in, 16)
            sp.dma_start(w_up_lat[:, 192:192 + D], io["W_vu"]).then_inc(weights_in, 16)
            sp.dma_start(w_ropek[:], io["W_ropek"].rearrange("p (h d) -> p h d", h=H)).then_inc(weights_in, 16)
            sp.dma_start(w_mla_o[:], io["W_o"]).then_inc(weights_in, 16)
            for n, name in enumerate(("bq", "bk", "bv", "w_ln1", "w_ln2")):
                sp.dma_start(cols[:, n:n + 1], io[name].rearrange("(p o) -> p o", o=1)).then_inc(weights_in, 16)
            sp.dma_start(bo_all[:], io["bo"].rearrange("(o d) -> o d", o=1).broadcast_to((P, D))).then_inc(weights_in, 16)
            sp.wait_ge(zeroed, 1)
            for i in range(2):
                for hp in range(2):
                    for r in range(2):
                        row = SLOT * hp + SHIFT_ROW + r
                        sp.dma_start(k_stack[i][row:row + 1, :, :],
                                     rows_dram[0:1, :].rearrange("o (a n) -> o a n", n=S)).then_inc(k_ones_in, 16)

            for step in steps:
                kind, b = step[0], step[1] if len(step) > 1 else 0
                if kind == "KD":
                    sp.wait_ge(misc_drained, misc_no[("LK", b)])
                    if b == 0:
                        sp.wait_ge(zeroed, 4)
                    else:
                        sp.wait_ge(a_drained, a_no[("LS", b - 1, NLT - 1)])
                    for h in range(H):
                        rows = slice(HD * h, HD * h + HD)
                        sp.dma_start(k_diag[rows, h, :], kT[rows, :]).then_inc(k_diag_in, 16)
                if kind == "MB":
                    side = step[2]
                    n = 2 * b + side + 1
                    sp.wait_ge(split_ready, n)
                    for t in range(3):
                        sp.dma_start(parts_dram[b, side, t], parts[:, side, t, :]).then_inc(parts_out, 16)
                    sp.wait_ge(parts_out, 16 * 3 * n)
                    if b == 0:
                        sp.wait_ge(zeroed, 3)
                    if b >= 2:
                        sp.wait_ge(b_full, 2 * E_PER_B * (b - 1))
                    for t in range(TERMS):
                        for hp in range(2):
                            src = parts_dram[b, side, (K_PARTS, Q_PARTS)[side][t]].rearrange(
                                "(a e d) n -> e d a n", e=2, d=HD)[hp]
                            row = SLOT * hp + HD * t
                            dst = q_stack[b % 2][row:row + HD, :, hp, :] if side else k_stack[b % 2][row:row + HD, :, :]
                            sp.dma_start(dst, src).then_inc(stacks_in, 16)
                    if side:
                        for hp in range(2):
                            for r in range(2):
                                row = SLOT * hp + SHIFT_ROW + r
                                sp.dma_start(q_stack[b % 2][row:row + 1, :, hp, :],
                                             rows_dram[1:2, :].rearrange("o (a n) -> o a n", n=S)).then_inc(stacks_in, 16)
                if kind == "SHIFT":
                    sp.wait_ge(misc_drained, misc_no[step])
                    for r in range(2):
                        sp.dma_start(shift_dram[b, r], shift[:, r, :]).then_inc(shift_out, 16)
                    sp.wait_ge(shift_out, 32 * (b + 1))
                    for hp in range(2):
                        for r in range(2):
                            row = SLOT * hp + SHIFT_ROW + r
                            sp.dma_start(q_stack[b % 2][row:row + 1, :, hp, :],
                                         shift_dram[b, r].rearrange("(e a i) n -> e a (i n)", e=2, i=NT)[hp:hp + 1]
                                         ).then_inc(shift_in, 16)
            sp.wait_ge(a_full, a_no[("LS", B - 1, NLT - 1)])
            for n, name in enumerate(("Wg", "Wu", "Wd")):
                sp.dma_start(w_exp[:, 0, n, :], io[name + "_s"]).then_inc(experts_in, 16)
                sp.dma_start(w_exp[:, 1:, n, :], io[name + "_r"].rearrange("e p i -> p e i")).then_inc(experts_in, 16)
            sp.dma_start(w_router[:], io["W_router"]).then_inc(experts_in, 16)
            sp.dma_start(router_bias[:], io["routing_bias"].rearrange("(o d) -> o d", o=1).broadcast_to((P, ER))).then_inc(experts_in, 16)
            ov = out.rearrange("b (i p) d -> p b i d", p=P)
            for b in range(B):
                sp.wait_ge(sum_ready, b + 1)
                sp.dma_start(ov[:, b], x[:, b * NT:(b + 1) * NT, :]).then_inc(out_done, 16)
            sp.wait_ge(out_done, 16 * B)

        @block.gpsimd
        def _(pool):
            own = [0]

            def link(ins):
                own[0] += 1
                ins.then_inc(g_step, 1)
                pool.wait_ge(g_step, own[0])

            nc.gpsimd.memset(k_stack[0][:].bitcast(F32), 0.0)
            nc.gpsimd.memset(k_stack[1][:].bitcast(F32), 0.0).then_inc(zeroed, 1)
            nc.gpsimd.memset(q_stack[0][:].bitcast(F32), 0.0).then_inc(zeroed, 1)
            nc.gpsimd.memset(q_stack[1][:].bitcast(F32), 0.0).then_inc(zeroed, 1)
            nc.gpsimd.memset(k_diag[:], 0.0).then_inc(zeroed, 1)
            for step in steps:
                if step[0] == "LV":
                    _, b, l = step
                    t = NLT * b + l
                    pool.wait_ge(misc_drained, misc_no[step])
                    if t == 0:
                        pool.wait_ge(v_step, V_INIT)
                    if t >= 2:
                        pool.wait_ge(misc_full, misc_no[("LO", (t - 2) // NLT, (t - 2) % NLT)])
                    for j in range(len(LTILES[l])):
                        rows = slice(PAIR * j, PAIR * j + PAIR)
                        link(nc.gpsimd.tensor_copy(v_loc[rows, t % 2, j, :, 0:HD], v_tile[rows, t % 2, :, :]))
                    pool.sem_inc(v_spread, 1)
                if step[0] == "MB":
                    _, b, side = step
                    n = 2 * b + side + 1
                    pool.wait_ge(rot_ready, n)
                    if b:
                        pool.wait_ge(parts_out, 16 * 3 * (n - 2))
                    full = rot[:, side, :]
                    hi, mid, lo = (parts[:, side, t, :] for t in range(3))
                    link(nc.gpsimd.tensor_copy(hi, full))
                    link(nc.gpsimd.tensor_tensor(rest[:], full, hi, ALU.subtract))
                    link(nc.gpsimd.tensor_copy(mid, rest[:]))
                    nc.gpsimd.tensor_tensor(lo, rest[:], mid, ALU.subtract).then_inc(split_ready, 1)
                    pool.wait_ge(split_ready, n)

        @block.scalar
        def _(act):
            act.wait_ge(sqrt_in, 1)
            nc.scalar.activation(nrm[:, 0, :], nrm[:, 0, :], ACT.Sqrt).then_inc(sqrt_out, 1)
            nc.scalar.activation(nrm[:, 1, :], nrm[:, 1, :], ACT.Sqrt).then_inc(sqrt_out, 1)
            act.wait_ge(weights_in, 16 * 18)

            def drained(step, dst, src, bias=None, scale=None):
                act.wait_ge(misc_full, misc_no[step])
                if bias is None and scale is None:
                    ins = nc.scalar.copy(dst, src)
                elif bias is None:
                    ins = nc.scalar.activation(dst, src, ACT.Copy, scale=scale)
                else:
                    ins = nc.scalar.activation(dst, src, ACT.Identity, bias=bias)
                ins.then_inc(misc_drained, 1)

            for step in steps:
                kind, b = step[0], step[1] if len(step) > 1 else 0
                if kind == "XT":
                    dst = xrT[:, b, :] if step[2] else xnT[:, b % 2, 0:S]
                    drained(step, dst, misc[:], scale=cols[:, 3:4] if step[2] else None)
                elif kind == "LQ":
                    if b >= 2:
                        act.wait_ge(a_full, a_no[("LS", b - 2, NLT - 1)])
                    drained(step, qT[:, b % 2, 0:S], misc[:], bias=cols[:, 0:1])
                elif kind == "LK":
                    if b:
                        act.wait_ge(k_diag_in, 16 * H * b)
                    drained(step, kT[:, 0:S], misc[:], bias=cols[:, 1:2])
                elif kind == "MV":
                    if b >= 2:
                        act.wait_ge(pv_done, E_PER_B * (b - 1))
                    drained(step, v_mla[:, b % 2, :, :, 0:HD],
                            misc[:].rearrange("p (i h d) -> p i h d", i=NT, h=H))
                elif kind == "YT":
                    drained(step, yT_mla, misc[:])
                elif kind == "LV":
                    t = NLT * b + step[2]
                    if t >= 2:
                        act.wait_ge(v_spread, t - 1)
                    np_ = PAIR * len(LTILES[step[2]])
                    drained(step, v_tile[0:np_, t % 2, :, :],
                            misc[0:np_, 0:D].rearrange("p (h d) -> p h d", h=H))
                elif kind == "LS":
                    t = NLT * b + step[2]
                    np_ = PAIR * len(LTILES[step[2]])
                    act.wait_ge(a_drained, a_no[step])
                    nc.scalar.activation(p_loc[0:np_, t % 2, :], p_loc[0:np_, t % 2, :], ACT.Exp,
                                         scale=SCALE).then_inc(loc_exp, 1)
                elif kind == "LO":
                    drained(step, oT_loc[:], misc[:])
                elif kind == "X2T":
                    if b == 0:
                        act.wait_ge(sqrt_in, 2)
                        nc.scalar.activation(nrm[:, 0, :], nrm[:, 0, :], ACT.Sqrt).then_inc(sqrt_out, 1)
                    drained(step, x2T[:, b, :], misc[:], scale=cols[:, 4:5])
                elif kind == "E":
                    _, b, g, j = step
                    n = e_no[step]
                    if n > P_RING:
                        act.wait_ge(pv_done, n - P_RING)
                    for half in range(2):
                        act.wait_ge(b_full, 2 * (n - 1) + half + 1)
                        nc.scalar.activation(p_mla[:, n % P_RING, 2 * half:2 * half + 2, j * P:],
                                             bank_b[half][:, :, j * P:], ACT.Exp, scale=SCALE).then_inc(b_drained, 1)
                elif kind == "PV" and step[3] == NT - 1:
                    _, b, g, _ = step
                    act.wait_ge(pv_done, pv_no[step])
                    if b and g == 0:
                        act.wait_ge(misc_full, misc_no[("X1", b - 1)])
                    nc.scalar.copy(oT_mla[:, g, :], bank_c[:]).then_inc(c_drained, 1)
                elif kind == "ROUTE":
                    act.wait_ge(probs_in, 1)
                    nc.scalar.activation(rt[:, 1, :, 0:ER], rt[:, 0, :, 0:ER], ACT.Sigmoid).then_inc(probs_out, 1)
                elif kind == "GU":
                    n = gu_no[step]
                    act.wait_ge(b_full, 2 * E_PER_B * B + n)
                    if n > 2:
                        act.wait_ge(hid_ready, n - 2)
                    nc.scalar.activation(gate[n % 2], bank_b[n % 2][:, 0, :], ACT.Silu).then_inc(gate_ready, 1)

        @block.vector
        def _(dve):
            own = [0]

            def link(ins):
                own[0] += 1
                ins.then_inc(v_step, 1)
                dve.wait_ge(v_step, own[0])

            nc.vector.memset(misc[:], 0.0)
            nc.vector.memset(bank_c[:], 0.0)
            nc.vector.memset(xnT[:, :, S:], 0.0)
            nc.vector.memset(attnT[:, S:], 0.0)
            for n in range(2):
                link(nc.vector.memset(v_loc[:, n, :, :, :], 0.0))
                for j in range(4):
                    nc.vector.memset(v_loc[PAIR * j:PAIR * j + PAIR, n, j, :, HD:], 1.0)
            link(nc.vector.memset(v_mla[:, :, :, :, HD:], 1.0))
            for b in range(B):
                dve.wait_ge(x_in[b], 16)
                for t in range(b * NT, b * NT + NT):
                    last = nc.vector.bn_stats(stats[:, t, :], x[:, t, :])
            link(last)
            for t in range(TILES):
                last = nc.vector.bn_aggr(mv[:, t, :], stats[:, t, :])
            link(last)
            link(nc.vector.tensor_scalar(nrm[:, 0, :], mv[:, :, 1], LN_EPS, None, ALU.add))
            link(nc.vector.reciprocal(nrm[:, 2, :], nrm[:, 0, :]))
            nc.vector.tensor_tensor(nrm[:, 1, :], mv[:, :, 1], nrm[:, 2, :], ALU.mult).then_inc(sqrt_in, 1)
            dve.wait_ge(sqrt_out, 2)
            link(nc.vector.reciprocal(nrm[:, 2, :], nrm[:, 0, :]))
            link(nc.vector.tensor_scalar(nrm[:, 1, :], nrm[:, 1, :], RMS_EPS, None, ALU.add))
            link(nc.vector.reciprocal(nrm[:, 3, :], nrm[:, 1, :]))
            for b in range(B):
                for t in range(b * NT, b * NT + NT):
                    last = nc.vector.tensor_scalar(xn[:, t, :], x[:, t, :], mv[:, t, 0:1], nrm[:, 2, t:t + 1],
                                                   ALU.subtract, ALU.mult)
                last.then_inc(xn_ready, 1)
                dve.wait_ge(xn_ready, 2 * b + 1)
                for t in range(b * NT, b * NT + NT):
                    last = nc.vector.tensor_scalar(xr[:, t, :], xn[:, t, :], nrm[:, 3, t:t + 1], None, ALU.mult)
                last.then_inc(xn_ready, 1)
            dve.wait_ge(consts_in, 16 * 4)
            dve.wait_ge(weights_in, 16 * 18)
            nc.vector.tensor_scalar(kT[:, S:], xnT[:, 0, S:], cols[:, 1:2], None, ALU.add)
            for n in range(2):
                nc.vector.tensor_scalar(qT[:, n, S:], xnT[:, 0, S:], cols[:, 0:1], None, ALU.add)
            for t in range(TILES):
                last = nc.vector.tensor_tensor(x[:, t, :], x[:, t, :], bo_all[:], ALU.add)
            last.then_inc(xres_ready, 1)

            def outputs(step, dst, np_, den):
                o = misc[0:np_, :].rearrange("p (h r) -> p h r", h=H)
                dve.wait_ge(misc_full, misc_no[step])
                link(nc.vector.reciprocal(den[0:np_, :], o[:, :, HD]))
                nc.vector.tensor_tensor(dst.rearrange("p (h d) -> p h d", h=H), o[:, :, 0:HD],
                                        den[0:np_, :].unsqueeze(2).broadcast_to((np_, H, HD)), ALU.mult).then_inc(misc_drained, 1)

            for step in steps:
                kind, b = step[0], step[1] if len(step) > 1 else 0
                if kind == "WF":
                    dve.wait_ge(misc_full, misc_no[step])
                    m = misc[:, 0:192].rearrange("p (n h d) -> p n h d", n=3, h=H)
                    half = HH // 2
                    nc.vector.memset(w_mla[:, :, 1, :, 0:HH], 0.0)
                    nc.vector.tensor_copy(w_mla[:, 0, 0, :, 0:HH], m[:, 0])
                    nc.vector.tensor_copy(w_mla[:, 1, 0, :, 0:HH], m[:, 1])
                    nc.vector.tensor_copy(w_mla[:, 0, 0, :, HH:], w_ropek[:])
                    nc.vector.tensor_copy(w_mla[:, 1, 0, :, HH:], m[:, 2])
                    nc.vector.tensor_copy(w_mla[:, 0, 1, :, HH:HH + half], w_ropek[:, :, half:])
                    nc.vector.tensor_copy(w_mla[:, 0, 1, :, HH + half:], w_ropek[:, :, 0:half])
                    nc.vector.tensor_copy(w_mla[:, 1, 1, :, HH:HH + half], m[:, 2, :, half:])
                    nc.vector.tensor_copy(w_mla[:, 1, 1, :, HH + half:], m[:, 2, :, 0:half])
                    nc.vector.tensor_copy(w_mla_v[:], misc[:, 192:192 + D]).then_inc(misc_drained, 1)
                elif kind in ("MA", "MB"):
                    side, which = step[2], int(kind == "MB")
                    if b and which == 0:
                        dve.wait_ge(split_ready, 2 * (b - 1) + side + 1)
                    dve.wait_ge(misc_full, misc_no[step])
                    dst = turned[:] if which else rot[:, side, :]
                    nc.vector.tensor_tensor(dst, misc[:], rope[:, which, :],
                                            ALU.mult).then_inc(misc_drained, 1)
                    if which:
                        dve.wait_ge(misc_drained, misc_no[step])
                        nc.vector.tensor_tensor(rot[:, side, :], rot[:, side, :], turned[:],
                                                ALU.add).then_inc(rot_ready, 1)
                elif kind == "S":
                    i, heads = UNITS[step[2]]
                    w = (i + 1) * P
                    dve.wait_ge(a_full, a_no[step])
                    for h in heads:
                        pass
                    src = bank_a[a_no[step] % 2][:, 0:w * len(heads)].rearrange("p (h k) -> p h k", k=w)
                    if len(heads) == 1:
                        dst = neg_max[:, heads[0] % 2, heads[0] // 2, i:i + 1]
                    else:
                        a0, na = heads[0] // 2, len(heads) // 2
                        dst = neg_max[:, :, a0:a0 + na, i].rearrange("p e a -> p a e")
                        src = src.rearrange("p (a e) k -> p a e k", e=2)
                    nc.vector.tensor_reduce(dst, src, AX.X, ALU.max, negate=True).then_inc(a_drained, 1)
                elif kind == "SHIFT":
                    dve.wait_ge(misc_full, misc_no[step])
                    if b:
                        dve.wait_ge(shift_out, 32 * b)
                    link(nc.vector.tensor_copy(shift[:, 0, :], misc[0:H * NT, 0:P]))
                    nc.vector.tensor_tensor(shift[:, 1, :], misc[0:H * NT, 0:P], shift[:, 0, :],
                                            ALU.subtract).then_inc(misc_drained, 1)
                elif kind == "LS":
                    t = NLT * b + step[2]
                    np_ = PAIR * len(LTILES[step[2]])
                    sc = bank_a[a_no[step] % 2][0:np_, :].rearrange("p (h k) -> p h k", h=H)
                    dve.wait_ge(a_full, a_no[step])
                    link(nc.vector.tensor_reduce(row_max[0:np_, :], sc, AX.X, ALU.max))
                    nc.vector.tensor_tensor(p_loc[0:np_, t % 2, :].rearrange("p (h k) -> p h k", h=H), sc,
                                            row_max[0:np_, :].unsqueeze(2).broadcast_to((np_, H, PAIR)),
                                            ALU.subtract).then_inc(a_drained, 1)
                elif kind == "LO":
                    t = NLT * b + step[2]
                    np_ = PAIR * len(LTILES[step[2]])
                    dve.wait_ge(loc_exp, ls_no[("LS", b, step[2])])
                    if t >= 2:
                        dve.wait_ge(misc_full, misc_no[("LO", (t - 2) // NLT, (t - 2) % NLT)])
                    nc.vector.transpose(pT_loc[0:np_, t % 2, :], p_loc[0:np_, t % 2, :]).then_inc(loc_turned, 1)
                elif kind == "LY":
                    np_ = PAIR * len(LTILES[step[2]])
                    outputs(step, y_loc[0:np_, :], np_, rden)
                elif kind == "LT":
                    tile = LTILES[step[2]]
                    dve.wait_ge(misc_full, misc_no[step])
                    if b and step[2] == 0:
                        dve.wait_ge(misc_full, misc_no[("LW", b - 1)])
                    for n, (g0, ng, first, stp) in enumerate(runs(tile)):
                        dst = attnT[:, tokens(first, stp, PAIR * ng)]
                        src = misc[:, g0 * PAIR:(g0 + ng) * PAIR]
                        if tile[0][0] == "local":
                            last = nc.vector.tensor_scalar(dst, src, cols[:, 2:3], None, ALU.add)
                        else:
                            if step[2] == S // P and n == 0:
                                dve.wait_ge(misc_drained, misc_no[("LT", b, S // P - 1)])
                            last = nc.vector.scalar_tensor_tensor(out=dst, in0=src, scalar=cols[:, 2:3], in1=dst,
                                                                  op0=ALU.add, op1=ALU.add)
                    last.then_inc(misc_drained, 1)
                elif kind == "LW":
                    dve.wait_ge(misc_full, misc_no[step])
                    xb = x[:, b * NT:(b + 1) * NT, :]
                    nc.vector.tensor_tensor(xb, misc[:].rearrange("p (i d) -> p i d", i=NT), xb,
                                            ALU.add).then_inc(misc_drained, 1)
                elif kind == "Y":
                    outputs(step, y_mla[:, step[2], :], P, rden_mla)
                elif kind == "X1":
                    dve.wait_ge(misc_full, misc_no[step])
                    tb = slice(b * NT, (b + 1) * NT)
                    nc.vector.tensor_tensor(x1[:, tb, :], misc[:].rearrange("p (i d) -> p i d", i=NT), xn[:, tb, :],
                                            ALU.add).then_inc(misc_drained, 1)
                elif kind == "X2T" and b == 0:
                    dve.wait_ge(misc_drained, misc_no[("LW", B - 1)])
                    for t in range(TILES):
                        last = nc.vector.tensor_tensor_reduce(xn[:, t, :], x1[:, t, :], x1[:, t, :], 1.0 / D, 0.0,
                                                              ALU.mult, ALU.add, nrm[:, 0, t:t + 1])
                    last.then_inc(sqrt_in, 1)
                    for t in range(TILES):
                        last = nc.vector.tensor_tensor(x[:, t, :], x[:, t, :], x1[:, t, :], ALU.add)
                    dve.wait_ge(sqrt_out, 3)
                    link(nc.vector.tensor_scalar(nrm[:, 1, :], nrm[:, 0, :], RMS_EPS, None, ALU.add))
                    link(nc.vector.reciprocal(nrm[:, 2, :], nrm[:, 1, :]))
                    for t in range(TILES):
                        ins = nc.vector.tensor_scalar(xn[:, t, :], x1[:, t, :], nrm[:, 2, t:t + 1], None, ALU.mult)
                        if t % NT == NT - 1:
                            ins.then_inc(xn_ready, 1)
                elif kind == "ROUTE":
                    dve.wait_ge(misc_full, misc_no[step])
                    dve.wait_ge(experts_in, 16 * 8)
                    nc.vector.tensor_tensor(rt[:, 0, :, 0:ER], misc[:, 0:TILES * ER].rearrange("p (t e) -> p t e", e=ER),
                                            router_bias[:].unsqueeze(1).broadcast_to((P, TILES, ER)), ALU.add).then_inc(misc_drained, 1)
                    nc.vector.memset(rt[:, 1, :, ER:], -1.0).then_inc(probs_in, 1)
                    dve.wait_ge(misc_drained, misc_no[step])
                    dve.wait_ge(probs_out, 1)
                    for t in range(TILES):
                        last = nc.vector.max(rt[:, 2, t, :], rt[:, 1, t, :])
                    link(last)
                    for t in range(TILES):
                        last = nc.vector.max_index(rt_idx[:, t, :], rt[:, 2, t, :], rt[:, 1, t, :])
                    link(last)
                    link(nc.vector.tensor_copy(rt[:, 3, :, :], rt_idx[:]))
                    link(nc.vector.tensor_tensor(rt_sum[:, 0, :], rt[:, 2, :, 0], rt[:, 2, :, 1], ALU.add))
                    link(nc.vector.reciprocal(rt_sum[:, 1, :], rt_sum[:, 0, :]))
                    link(nc.vector.tensor_tensor(rt[:, 2, :, 0:2], rt[:, 2, :, 0:2],
                                                 rt_sum[:, 1, :].unsqueeze(2).broadcast_to((P, TILES, 2)), ALU.mult))
                    for n in range(2):
                        link(nc.vector.tensor_tensor(rt[:, 4 + n, :, :], rt[:, 3, :, n:n + 1].broadcast_to((P, TILES, 8)),
                                                     expert_ids[:].unsqueeze(1).broadcast_to((P, TILES, 8)), ALU.is_equal))
                        link(nc.vector.tensor_tensor(rt[:, 4 + n, :, :], rt[:, 4 + n, :, :],
                                                     rt[:, 2, :, n:n + 1].broadcast_to((P, TILES, 8)), ALU.mult))
                    link(nc.vector.tensor_tensor(rt[:, 4, :, :], rt[:, 4, :, :], rt[:, 5, :, :], ALU.add))
                elif kind == "GU":
                    n = gu_no[step]
                    dve.wait_ge(gate_ready, n)
                    if n > 2:
                        dve.wait_ge(a_full, a_no[("DOWN",) + divmod(n - 3, NE)])
                    nc.vector.tensor_tensor(hid[n % 2], bank_b[n % 2][:, 1, :], gate[n % 2],
                                            ALU.mult).then_inc(hid_ready, 1)
                elif kind == "ADD":
                    _, c, e = step
                    n = a_no[("DOWN", c, e)]
                    dve.wait_ge(a_full, n)
                    xc = x[:, c * NT:(c + 1) * NT, :]
                    down = bank_a[n % 2][:].rearrange("p (i d) -> p i d", i=NT)
                    if e == 0:
                        ins = nc.vector.tensor_tensor(xc, down, xc, ALU.add)
                    else:
                        dve.wait_ge(a_drained, n - 1)
                        for i in range(NT):
                            t = c * NT + i
                            ins = nc.vector.scalar_tensor_tensor(out=x[:, t, :], in0=down[:, i, :],
                                                                 scalar=rt[:, 4, t, e - 1:e], in1=x[:, t, :],
                                                                 op0=ALU.mult, op1=ALU.add)
                    ins.then_inc(a_drained, 1)
                    if e == NE - 1:
                        dve.wait_ge(a_drained, n)
                        dve.sem_inc(sum_ready, 1)

        @block.tensor
        def _(pe):
            def open_misc(step):
                n = misc_no[step]
                if n > 1:
                    pe.wait_ge(misc_drained, n - 1)
                return n

            def open_a(step):
                n = a_no[step]
                if n > 2:
                    pe.wait_ge(a_drained, n - 2)
                return bank_a[n % 2]

            pe.wait_ge(v_step, V_INIT)
            pe.wait_ge(consts_in, 16 * 4)
            pe.wait_ge(weights_in, 16 * 18)
            for step in steps:
                kind, b = step[0], step[1] if len(step) > 1 else 0
                if kind == "WF":
                    for n, (down, c0, c1) in enumerate(((0, 0, 64), (1, 64, 128), (1, 128, 192), (0, 192, 192 + D))):
                        last = nc.tensor.matmul(misc[:, c0:c1], w_down_lat[:, down, :], w_up_lat[:, c0:c1],
                                                start=True, stop=True)
                    last.then_inc(misc_full, 1)
                elif kind in ("XT", "X2T"):
                    second = kind == "X2T"
                    pe.wait_ge(xn_ready, 2 * B + b + 1 if second else 2 * b + 1 + step[2])
                    open_misc(step)
                    src = xn if second or not step[2] else xr
                    for i in range(NT):
                        last = nc.tensor.transpose(misc[:, i * P:(i + 1) * P], src[:, b * NT + i, :], eye[:])
                    last.then_inc(misc_full, 1)
                elif kind in ("LQ", "LK"):
                    pe.wait_ge(misc_drained, misc_no[("XT", b, 0)])
                    open_misc(step)
                    nc.tensor.matmul(misc[:], w_attn[:, int(kind == "LK"), :], xnT[:, b % 2, 0:S], start=True,
                                     stop=True).then_inc(misc_full, 1)
                elif kind in ("MA", "MB"):
                    open_misc(step)
                    pe.wait_ge(misc_drained, misc_no[("XT", b, 1)])
                    nc.tensor.matmul(misc[:], w_mla[:, step[2], int(kind == "MB"), :, :], xrT[:, b, :], start=True,
                                     stop=True).then_inc(misc_full, 1)
                elif kind == "MV":
                    open_misc(step)
                    for i in range(NT):
                        last = nc.tensor.matmul(misc[:, i * D:(i + 1) * D], xrT[:, b, i * P:(i + 1) * P], w_mla_v[:],
                                                start=True, stop=True)
                    last.then_inc(misc_full, 1)
                elif kind == "S":
                    i, heads = UNITS[step[2]]
                    w = (i + 1) * P
                    if step[2] == 0:
                        pe.wait_ge(k_ones_in, 16 * 8)
                        pe.wait_ge(stacks_in, BOTH_IN * (b + 1))
                    bank = open_a(step)
                    for n, h in enumerate(heads):
                        nc.tensor.matmul(bank[:, n * w:(n + 1) * w], q_stack[b % 2][:, h // 2, h % 2, i * P:(i + 1) * P],
                                         k_stack[b % 2][:, h // 2, 0:w], start=True, stop=False, skip_group_check=True)
                        last = nc.tensor.matmul(bank[:, (n + 1) * w - P:(n + 1) * w], eye16, causal16,
                                                start=False, stop=True, skip_group_check=True)
                    last.then_inc(a_full, 1)
                elif kind == "SHIFT":
                    pe.wait_ge(a_drained, a_no[("S", b, len(UNITS) - 1)])
                    open_misc(step)
                    nc.tensor.transpose(misc[0:H * NT, 0:P], neg_max[:].rearrange("p e a i -> p (e a i)"),
                                        eye[:]).then_inc(misc_full, 1)
                elif kind == "E":
                    _, b, g, j = step
                    n = e_no[step]
                    if g == 0 and j == 0:
                        pe.wait_ge(shift_in, 64 * (b + 1))
                    for half in range(2):
                        if n > 1:
                            pe.wait_ge(b_drained, 2 * (n - 2) + half + 1)
                        for m in range(2):
                            h = 4 * g + 2 * half + m
                            nc.tensor.matmul(bank_b[half][:, m, j * P:], k_stack[b % 2][:, h // 2, j * P:(j + 1) * P],
                                             q_stack[b % 2][:, h // 2, h % 2, j * P:], start=True, stop=False,
                                             skip_group_check=True)
                            last = nc.tensor.matmul(bank_b[half][:, m, j * P:(j + 1) * P], eye16, causalT16,
                                                    start=False, stop=True, skip_group_check=True)
                        last.then_inc(b_full, 1)
                elif kind == "PV":
                    _, b, g, j = step
                    n = pv_no[step]
                    pe.wait_ge(b_drained, 2 * n)
                    pe.wait_ge(misc_drained, misc_no[("MV", b)])
                    if j == 0 and n > 1:
                        pe.wait_ge(c_drained, (n - 1) // NT)
                    for m in range(4):
                        last = nc.tensor.matmul(bank_c[32 * m:32 * m + HD + 1, j * P:], v_mla[:, b % 2, j, 4 * g + m, :],
                                                p_mla[:, n % P_RING, m, j * P:], start=(j == 0), stop=(j == NT - 1),
                                                skip_group_check=True)
                    last.then_inc(pv_done, 1)
                elif kind == "Y":
                    if step[2] == 0:
                        pe.wait_ge(c_drained, (b + 1) * (H // 4))
                    open_misc(step)
                    for g in range(4):
                        last = nc.tensor.transpose(misc[:, g * P:(g + 1) * P], oT_mla[:, g, step[2] * P:(step[2] + 1) * P],
                                                   eye[:])
                    last.then_inc(misc_full, 1)
                elif kind == "YT":
                    pe.wait_ge(misc_drained, misc_no[("Y", b, NT - 1)])
                    open_misc(step)
                    for i in range(NT):
                        last = nc.tensor.transpose(misc[:, i * P:(i + 1) * P], y_mla[:, i, :], eye[:])
                    last.then_inc(misc_full, 1)
                elif kind == "X1":
                    pe.wait_ge(misc_drained, misc_no[("YT", b)])
                    open_misc(step)
                    for i in range(NT):
                        last = nc.tensor.matmul(misc[:, i * D:(i + 1) * D], yT_mla[:, i * P:(i + 1) * P], w_mla_o[:],
                                                start=True, stop=True)
                    last.then_inc(misc_full, 1)
                elif kind == "LV":
                    open_misc(step)
                    for j, (_, first, stp) in enumerate(LTILES[step[2]]):
                        last = nc.tensor.matmul(misc[PAIR * j:PAIR * j + PAIR, 0:D], xnT[:, b % 2, tokens(first, stp)],
                                                w_attn[:, 2, :], start=True, stop=True, skip_group_check=True)
                    last.then_inc(misc_full, 1)
                elif kind == "LS":
                    if step[2] == 0:
                        pe.wait_ge(k_diag_in, 16 * H * (b + 1))
                        pe.wait_ge(misc_drained, misc_no[("LQ", b)])
                        if b == 0:
                            pe.wait_ge(xres_ready, 1)
                    t = NLT * b + step[2]
                    if t >= 2:
                        pe.wait_ge(loc_turned, t - 1)
                    np_ = PAIR * len(LTILES[step[2]])
                    bank = open_a(step)
                    nc.tensor.matmul(bank[0:np_, :], eye16[:, 0:np_], pair16, start=True, stop=False, skip_group_check=True)
                    for j, (_, first, stp) in enumerate(LTILES[step[2]]):
                        last = nc.tensor.matmul(bank[PAIR * j:PAIR * j + PAIR, :], qT[:, b % 2, tokens(first, stp)],
                                                k_diag[:, :, tokens(first, stp)], start=False, stop=True,
                                                skip_group_check=True)
                    last.then_inc(a_full, 1)
                elif kind == "LO":
                    t = NLT * b + step[2]
                    np_ = PAIR * len(LTILES[step[2]])
                    pe.wait_ge(loc_turned, lo_no[step])
                    pe.wait_ge(v_spread, t + 1)
                    open_misc(step)
                    for h in range(0, H, 4):
                        for j in range(len(LTILES[step[2]])):
                            for m in range(4):
                                c = h * PAIR + j * PAIR
                                last = nc.tensor.matmul(misc[32 * m:32 * m + HD + 1, c:c + PAIR],
                                                        v_loc[0:np_, t % 2, j, h + m, :],
                                                        pT_loc[0:np_, t % 2, (h + m) * PAIR:(h + m + 1) * PAIR],
                                                        start=True, stop=True, skip_group_check=True)
                    last.then_inc(misc_full, 1)
                elif kind == "LY":
                    np_ = PAIR * len(LTILES[step[2]])
                    pe.wait_ge(misc_drained, misc_no[("LO", b, step[2])])
                    open_misc(step)
                    for g in range(4):
                        last = nc.tensor.transpose(misc[0:np_, g * P:(g + 1) * P], oT_loc[:, g * P:g * P + np_], eye[:])
                    last.then_inc(misc_full, 1)
                elif kind == "LT":
                    np_ = PAIR * len(LTILES[step[2]])
                    pe.wait_ge(misc_drained, misc_no[("LY", b, step[2])])
                    open_misc(step)
                    nc.tensor.transpose(misc[:, 0:np_], y_loc[0:np_, :], eye[0:np_, 0:np_]).then_inc(misc_full, 1)
                elif kind == "LW":
                    pe.wait_ge(misc_drained, misc_no[("LT", b, NLT - 1)])
                    open_misc(step)
                    for i in range(NT):
                        last = nc.tensor.matmul(misc[:, i * D:(i + 1) * D], attnT[:, i * P:(i + 1) * P], w_attn[:, 3, :],
                                                start=True, stop=True)
                    last.then_inc(misc_full, 1)
                elif kind == "ROUTE":
                    pe.wait_ge(experts_in, 16 * 8)
                    open_misc(step)
                    for t in range(TILES):
                        last = nc.tensor.matmul(misc[:, t * ER:(t + 1) * ER], x2T[:, t // NT, (t % NT) * P:(t % NT + 1) * P],
                                                w_router[:], start=True, stop=True)
                    last.then_inc(misc_full, 1)
                elif kind == "GU":
                    _, c, e = step
                    n = gu_no[step]
                    if n <= 2:
                        pe.wait_ge(b_drained, 2 * E_PER_B * B)
                    else:
                        pe.wait_ge(hid_ready, n - 2)
                    for m in range(2):
                        last = nc.tensor.matmul(bank_b[n % 2][:, m, :], w_exp[:, e, m, :], x2T[:, c, :], start=True, stop=True)
                    last.then_inc(b_full, 1)
                elif kind == "DOWN":
                    _, c, e = step
                    n = gu_no[("GU", c, e)]
                    bank = open_a(step)
                    pe.wait_ge(hid_ready, n)
                    for i in range(NT):
                        last = nc.tensor.matmul(bank[:, i * D:(i + 1) * D], hid[n % 2][:, i * P:(i + 1) * P],
                                                w_exp[:, e, 2, :], start=True, stop=True)
                    last.then_inc(a_full, 1)


_TURNED = ("Wq", "Wk", "Wv", "Wo", "W_kvd", "W_qd")
_NAMES = ["L0_attn_" + n for n in ("x", "Wq", "bq", "Wk", "bk", "Wv", "bv", "Wo", "bo")] + ["L0_ffn_" + n for n in (
    "w_ln1", "w_ln2", "W_kvd", "W_qd", "W_ku", "W_qu", "W_vu", "W_ropeq", "W_ropek", "W_o", "Wg_s", "Wu_s", "Wd_s",
    "Wg_r", "Wu_r", "Wd_r", "W_router", "routing_bias")]


def kernel(**inputs):
    import numpy as _np
    import concourse.bacc as _bacc
    from concourse import mybir as _mybir
    from concourse.bass_utils import run_bass_kernel_spmd as _run

    nc = _bacc.Bacc("TRN2", target_bir_lowering=False, num_devices=1)
    laid = {}
    for full in _NAMES:
        name = full.split("_", 2)[2]
        a = _np.asarray(inputs[full])
        laid[name] = _np.ascontiguousarray(a.T if name in _TURNED else a)
    laid.update(constants())
    arrays, io = {}, {}
    for name, a in laid.items():
        arrays[f"in_{name}"] = a
        io[name] = nc.dram_tensor(f"in_{name}", a.shape, _mybir.dt.from_np(a.dtype), kind="ExternalInput").ap()
    out = nc.dram_tensor("out_0", (B, S, D), _mybir.dt.float32, kind="ExternalOutput").ap()
    build(nc, io, out)
    r = _run(nc, [arrays], core_ids=[0])
    return r.results[0]["out_0"]
```

```python
from contextlib import ExitStack

import numpy as np

import concourse.bass as bass
from concourse import mybir

F32 = mybir.dt.float32
BF16 = mybir.dt.bfloat16
U32 = mybir.dt.uint32
ALU = mybir.AluOpType
ACT = mybir.ActivationFunctionType
AX = mybir.AxisListType

P = 128
B = 4
S = 512
D = 128
H = 16
HD = 8
HH = HD // 2
LAT = D // 4
NT = S // P
TILES = B * NT
CHUNK = 16
DIL = 3
PAIR = 2 * CHUNK
LPH = -(-S // DIL)
LPH_PAIRS = -(-LPH // PAIR)
SX = LPH_PAIRS * PAIR * DIL
ER = 7
NE = ER + 1
LN_EPS = 1e-5
RMS_EPS = 1e-5
SCALE = float(HD) ** -0.5
NEG = -1e30
TERMS = 6
STORES = (((0, 3, 0), (3, 2, 0), (5, 1, 0)),
          ((0, 3, 0), (3, 2, 1), (5, 1, 2)))
SLOT = 64
SHIFT_ROW = TERMS * HD
P_RING = 2


def columns(widths):
    at, found = 0, {}
    for name, width in widths:
        found[name] = slice(at, at + width)
        at += width
    return found, at


WIDE, WIDE_END = columns([(n, D) for n in ("Wq", "Wk", "Wv", "Wo")] + [("W_ropek", H * HH), ("W_o", D), ("W_router", ER)]
                         + [(n, 1) for n in ("bq", "bk", "bv", "w_ln1", "w_ln2")])
LATS, LAT_END = columns([("W_kvd", D), ("W_qd", D), ("W_ku", H * HH), ("W_qu", H * HH), ("W_ropeq", H * HH),
                         ("W_vu", D)])
BANKS = {"A": 2, "B": 3, "M": 2}

GROUPS = [[("local", g * PAIR, 1) for g in range(S // PAIR)],
          [("dilated", r + DIL * PAIR * g, DIL) for r in range(DIL) for g in range(LPH_PAIRS)]]
LTILES = [gs[n:n + 4] for gs in GROUPS for n in range(0, len(gs), 4)]
NLT = len(LTILES)


def score_units():
    units = []
    for i in range(NT):
        n = S // ((i + 1) * P)
        units += [(i, list(range(h, min(h + n, H)))) for h in range(0, H, n)]
    return units


UNITS = score_units()


def exp_units(g, j):
    n = max(1, 512 // (S - j * P))
    return [list(range(h, h + n)) for h in range(4 * g, 4 * g + 4, n)]


SPREAD = [
    {"maxima": (0.22, 0.88), "local": (0.06, 0.91), "project": (0.34, 0.57)},
    {"maxima": (0.12, 0.92), "local": (0, 0.82), "project": (0.4, 0.75), "stacks": (0.11, 0.11), "values": (0.03, 0.06)},
    {"maxima": (0.14, 0.92), "local": (0, 0.8), "project": (0.3, 0.65), "stacks": (0.02, 0.03), "values": (0.04, 0.07), "outputs": (0.08, 0.311), "norm": (0.371, 0.5)},
    {"maxima": (0.3, 0.84), "local": (0, 0.88), "stacks": (0.13, 0.16), "values": (0.01, 0.03), "outputs": (0, 0.275), "norm": (0.275, 0.5), "weights": (1, 1)},
    {"experts": (0.08, 1), "outputs": (0.01, 0.198), "norm": (0.238, 0.44)},
    {"outputs": (0, 0.246), "norm": (0.326, 0.54)},
]
EARLY = 24


def merged(*parts):
    keyed = [(lo + (hi - lo) * (k + 0.5) / len(one), n, k, step)
             for n, (one, lo, hi) in enumerate(parts) for k, step in enumerate(one)]
    return [x[3] for x in sorted(keyed, key=lambda x: x[:3])]


def plan():
    def project(b):
        return [("LN", b), ("XT", b, 0), ("LK", b), ("LQ", b), ("XT", b, 1), ("MA", b, 0), ("MB", b, 0),
                ("MA", b, 1), ("MB", b, 1)]

    def maxima(b):
        return [("S", b, u) for u in range(len(UNITS))] + [("SHIFT", b)]

    def latent(b):
        steps, late = [], []
        for g in range(H // 4):
            for j in range(NT):
                units = [("E", b, g, j, u) for u in range(len(exp_units(g, j)))]
                steps += units[:1] + late + units[1:]
                late = [("PV", b, g, j)]
        return steps + late

    def outputs(b):
        return [("Y", b, i) for i in range(NT)] + [("YT", b), ("X1", b)]

    def norm(b):
        return [("R2", b), ("R3", b), ("X2T", b), ("ROUTE", b), ("PICK", b)]

    def local(b):
        stages = [("LT", 4), ("LY", 3), ("LO", 2), ("LR", 1), ("LV", 1), ("LS", 0)]
        steps = []
        for k in range(NLT + 4):
            steps += [(stage, b, k - later) for stage, later in stages if 0 <= k - later < NLT]
            if k == NLT - 1 and b + 1 < B:
                steps.append(("KD", b + 1))
        return steps + [("LW", b)]

    def experts(batches):
        moe = [(c, e) for c in batches for e in range(NE)]
        steps = []
        for n in range(len(moe) + 2):
            if n < len(moe):
                steps.append(("GU",) + moe[n])
            if 1 <= n <= len(moe):
                steps.append(("DOWN",) + moe[n - 1])
            if n >= 2:
                steps.append(("ADD",) + moe[n - 2])
        return steps

    first = project(0)
    steps = first[:4] + [("KD", 0), ("WF",)] + first[4:] + [("STATS", 0), ("ST", 0), ("MV", 0)]
    at = SPREAD[0]
    steps += merged((maxima(0), *at["maxima"]), (local(0), *at["local"]),
                    ([("STATS", 1)] + project(1), *at["project"]))
    for b in range(B - 1):
        at = SPREAD[b + 1]
        window = [([("ST", b + 1)], *at["stacks"]), ([("MV", b + 1)], *at["values"]), (latent(b), 0, 1), (maxima(b + 1), *at["maxima"]),
                  (local(b + 1), *at["local"])]
        if b:
            window += [(outputs(b - 1), *at["outputs"]), (norm(b - 1), *at["norm"])]
        if b + 2 < B:
            window.append((project(b + 2), *at["project"]))
        else:
            window.append(([("WX",)], *at["weights"]))
        steps += merged(*window)
    at = SPREAD[B]
    moe = experts(range(B))
    steps += merged((latent(B - 1), 0, 1), (outputs(B - 2), *at["outputs"]), (norm(B - 2), *at["norm"]),
                    (moe[:EARLY], *at["experts"]))
    at = SPREAD[B + 1]
    steps += merged((outputs(B - 1), *at["outputs"]), (norm(B - 1), *at["norm"]), (moe[EARLY:], 0, 1))
    return steps


def bank_uses(step):
    kind = step[0]
    if kind in ("S", "LS", "DOWN"):
        return [("A", step)]
    if kind == "E":
        return [("B", step)]
    if kind == "GU":
        return [("B", step + (m,)) for m in range(2)]
    if kind in ("WF", "XT", "LQ", "LK", "MA", "MB", "MV", "SHIFT", "Y", "YT", "X1", "LV", "LO", "LY", "LT", "LW",
                "X2T", "ROUTE"):
        return [("M", step)]
    return []


class Ring:

    def __init__(self, steps, name):
        uses = [use for step in steps for ring, use in bank_uses(step) if ring == name]
        self.bank = {use: n % BANKS[name] for n, use in enumerate(uses)}
        self.count = {use: n // BANKS[name] + 1 for n, use in enumerate(uses)}


def numbers(steps, kinds):
    return {s: n + 1 for n, s in enumerate([s for s in steps if s[0] in kinds])}


def as_bf16(a):
    bits = np.ascontiguousarray(a, np.float32).view(np.uint32).astype(np.uint64)
    return ((bits + 0x7FFF + ((bits >> 16) & 1)) >> 16).astype(np.uint16)


def constants():
    eye = np.eye(P, dtype=np.float32)
    q, k = np.arange(P)[:, None], np.arange(P)[None, :]
    causal = np.where(k > q, NEG, 0.0).astype(np.float32)
    row_chunk = (np.arange(P)[:, None] // CHUNK) % 2
    col_chunk = (np.arange(H * PAIR)[None, :] // CHUNK) % 2
    pair = np.where(row_chunk != col_chunk, NEG, 0.0).astype(np.float32)
    inv = 1.0 / np.float32(10000.0) ** (np.arange(0, HH, 2, dtype=np.float32) / np.float32(HH))
    freqs = np.outer(np.arange(S, dtype=np.float32), inv.astype(np.float32))
    emb = np.concatenate([freqs, freqs], axis=-1)
    cos, sin = np.cos(emb).astype(np.float32), np.sin(emb).astype(np.float32)
    sin[:, :HH // 2] *= -1
    cosT = np.concatenate([np.ones((HH, S), np.float32), cos.T])
    sinT = np.concatenate([np.zeros((HH, S), np.float32), sin.T])
    return {
        "c_eye": eye,
        "c_masks": as_bf16(np.concatenate([eye, causal, causal.T, pair, np.zeros((P, S - P), np.float32), causal],
                                          axis=1)),
        "c_rope": np.stack([np.tile(np.repeat(t, H // 2, axis=0), (2, 1)) for t in (cosT, sinT)], axis=1),
        "c_rows": as_bf16(np.repeat([[1.0], [1.0], [0.0], [0.0]], H // 2 * S, axis=1)),
        "c_experts": np.broadcast_to(np.arange(8, dtype=np.float32), (P, 8)).copy(),
    }


def build(nc, io, out):
    steps = plan()
    rings = {name: Ring(steps, name) for name in BANKS}
    where = {use: (ring, rings[ring].bank[use], rings[ring].count[use])
             for step in steps for ring, use in bank_uses(step)}
    pv_no = numbers(steps, {"PV"})
    gu_no, add_no = numbers(steps, {"GU"}), numbers(steps, {"ADD"})
    single = [step for step in steps if step[0] == "S" and UNITS[step[2]][0] >= 2]
    downs = [step for step in steps if step[0] == "DOWN"]

    with ExitStack() as ctx:
        def sb(name, shape, dt=F32):
            return ctx.enter_context(nc.sbuf_tensor(name, shape, dt))

        def psum(name, shape):
            return ctx.enter_context(nc.psum_tensor(name, shape, F32))

        def sem(name):
            return ctx.enter_context(nc.semaphore(name))

        banks = {name: [psum(f"bank_{name}{i}", [P, 512]) for i in range(n)] for name, n in BANKS.items()}
        bank_c = psum("bank_c", [P, 512])

        eye = sb("eye", [P, P])
        masks = sb("masks", [P, 3 * P + 512 + S], BF16)
        eye16, causal16, causalT16, pair16 = (masks[:, 0:P], masks[:, P:2 * P], masks[:, 2 * P:3 * P],
                                              masks[:, 3 * P:3 * P + 512])
        masked16 = masks[:, 3 * P + 512:]
        rope = sb("rope", [P, 2, S])
        expert_ids = sb("expert_ids", [P, 8])
        wide = sb("wide", [P, WIDE_END])
        w_attn = wide[:, 0:4 * D].rearrange("p (n d) -> p n d", n=4)
        w_ropek = wide[:, WIDE["W_ropek"]].rearrange("p (h d) -> p h d", h=H)
        w_mla_o = wide[:, WIDE["W_o"]]
        w_router = wide[:, WIDE["W_router"]]
        cols = wide[:, WIDE["bq"].start:WIDE["w_ln2"].stop]
        lat_room = sb("lat_room", [P, LAT_END])
        lat = lat_room[0:LAT, :]
        w_down_lat = lat[:, 0:2 * D].rearrange("p (n d) -> p n d", n=2)
        w_up_lat = lat[:, 2 * D:]
        w_mla = sb("w_mla", [P, 2, 2, 2, HD, H // 2])
        w_mla_v = sb("w_mla_v", [P, D])
        on_all = sb("on_all", [P, D + ER])
        bo_all, router_bias = on_all[:, 0:D], on_all[:, D:]
        x = sb("x", [P, TILES, D])
        xn = sb("xn", [P, TILES, D])
        x1 = sb("x1", [P, TILES, D])
        xr = x1
        xnT = sb("xnT", [P, 2, SX])
        xrT = sb("xrT", [P, B, S])
        x2T = xrT
        stats = sb("stats", [P, TILES, 6])
        mv = sb("mv", [P, TILES, 2])
        nrm = sb("nrm", [P, 8, TILES])
        half = sb("half", [P, 2, TILES])
        qT = sb("qT", [P, 2, SX])
        kT = sb("kT", [P, SX])
        k_diag = sb("k_diag", [P, H, SX])
        v_loc = sb("v_loc", [P, 2, H, HD + 1])
        scratch = sb("scratch", [P, 512])
        s_loc = scratch
        sT_loc = sb("sT_loc", [P, 2, 512])
        pT_loc = sb("pT_loc", [P, H, P])
        row_max = sb("row_max", [P, H])
        oT_loc = sb("oT_loc", [P, 512])
        y_loc = sb("y_loc", [P, D])
        rden = sb("rden", [P, H])
        attnT = sb("attnT", [P, SX])
        rot = sb("rot", [P, 2, S])
        turned = scratch
        parts = sb("parts", [P, 2, 3, S], BF16)
        rest = sb("rest", [P, S])
        k_stack = [sb(f"k_stack{i}", [P, H // 2, S], BF16) for i in range(2)]
        q_stack = [sb(f"q_stack{i}", [P, H // 2, 2, S], BF16) for i in range(2)]
        differences = sb("differences", [P, S], BF16)
        neg_max = sb("neg_max", [P, 2, H // 2, NT])
        shift = sb("shift", [H * NT, 2, P], BF16)
        v_mla = sb("v_mla", [P, 2, NT, H, HD + 1])
        p_mla = sb("p_mla", [P, P_RING, 4, S])
        oT_mla = sb("oT_mla", [P, 4, S])
        y_mla = lat_room[:, 0:NT * D].rearrange("p (i d) -> p i d", i=NT)
        yT_mla = oT_mla[:, 0, :]
        rden_mla = sb("rden_mla", [P, H])
        late = k_diag[:].rearrange("p h n -> p (h n)")
        w_exp = late[:, 0:NE * 3 * D].rearrange("p (e n d) -> p e n d", e=NE, n=3)
        GATE0 = NE * 3 * D
        gate = [late[:, GATE0 + S * n:GATE0 + S * n + S] for n in range(2)]
        hid = [late[:, GATE0 + S * (n + 2):GATE0 + S * (n + 3)] for n in range(2)]
        rt = sb("rt", [P, 6, NT, 8])
        rt_idx = sb("rt_idx", [P, NT, 8], U32)
        rt_sum = sb("rt_sum", [P, 2, NT])
        expert_w = sb("expert_w", [P, TILES, 8])

        parts_dram = nc.dram_tensor("parts_dram", [B, 2, 2, TERMS, HD * H // 2, S], BF16, kind="Internal").ap()
        shift_dram = nc.dram_tensor("shift_dram", [B, 2, H * NT, P], BF16, kind="Internal").ap()
        rows_dram = io["c_rows"].bitcast(BF16)

        x_in = [sem(f"x_in{b}") for b in range(B)]
        eye_in, masks_in, rope_in = sem("eye_in"), sem("masks_in"), sem("rope_in")
        wide_in, lat_in = sem("wide_in"), sem("lat_in")
        late_in = sem("late_in")
        experts_in = sem("experts_in")
        k_ones_in = [sem(f"k_ones_in{i}") for i in range(2)]
        k_diag_in = sem("k_diag_in")
        parts_out = sem("parts_out")
        stacks_in = sem("stacks_in")
        shift_out = sem("shift_out")
        shift_in = sem("shift_in")
        out_done = sem("out_done")
        set_up = sem("set_up")
        pT_cleared = sem("pT_cleared")
        zeroed = sem("zeroed")
        diag_zeroed = sem("diag_zeroed")
        xn_ready = sem("xn_ready")
        x2_ready = sem("x2_ready")
        sqrt_in, sqrt_out = sem("sqrt_in"), sem("sqrt_out")
        full = {name: [sem(f"full_{name}{i}") for i in range(n)] for name, n in BANKS.items()}
        drained = {name: [sem(f"drained_{name}{i}") for i in range(n)] for name, n in BANKS.items()}
        pv_done, c_drained = sem("pv_done"), sem("c_drained")
        loc_turned = sem("loc_turned")
        loc_exp = sem("loc_exp")
        rot_ready = sem("rot_ready")
        rounded, rest_ready = sem("rounded"), sem("rest_ready")
        split_ready = sem("split_ready")
        gate_ready = sem("gate_ready")
        hid_ready = sem("hid_ready")
        added = sem("added")
        logits_ready, logits_exp = sem("logits_ready"), sem("logits_exp")
        tails_ready = sem("tails_ready")
        sum_ready = sem("sum_ready")
        v_step, g_step, s_step = sem("v_step"), sem("g_step"), sem("s_step")

        def tokens(first, step, n=PAIR):
            return slice(first, first + step * (n - 1) + 1, step)

        def runs(tile):
            found = []
            for n, (_, first, step) in enumerate(tile):
                if found and found[-1][2] + found[-1][1] * PAIR * step == first:
                    found[-1][1] += 1
                else:
                    found.append([n, 1, first, step])
            return found

        def bank_of(use):
            ring, i, _ = where[use]
            return banks[ring][i]

        def wait_full(eng, use):
            ring, i, n = where[use]
            eng.wait_ge(full[ring][i], n)

        def wait_drained(eng, use):
            ring, i, n = where[use]
            eng.wait_ge(drained[ring][i], n)

        def wait_free(eng, use):
            ring, i, n = where[use]
            if n > 1:
                eng.wait_ge(drained[ring][i], n - 1)

        def full_by(ins, use):
            ins.then_inc(full[where[use][0]][where[use][1]], 1)

        def drained_by(ins, use):
            ins.then_inc(drained[where[use][0]][where[use][1]], 1)

        E_PER_B = NT * (H // 4)
        STACK_IN = 16 * 6
        ACT_CLEARS = 12

        block = ctx.enter_context(nc.Block())

        @block.sync
        def _(sp):
            xv = io["x"].rearrange("b (i p) d -> p b i d", p=P)
            def load_x(b):
                sp.dma_start(x[:, b * NT:(b + 1) * NT, :], xv[:, b]).then_inc(x_in[b], 16)

            load_x(0)
            sp.dma_start(eye[:], io["c_eye"]).then_inc(eye_in, 16)
            sp.dma_start(wide[:], io["wide"]).then_inc(wide_in, 16)
            sp.dma_start(lat, io["lat"]).then_inc(lat_in, 16)
            sp.dma_start(masks[:], io["c_masks"].bitcast(BF16)).then_inc(masks_in, 16)
            sp.dma_start(rope[:], io["c_rope"]).then_inc(rope_in, 16)
            for b in range(1, B):
                load_x(b)
            sp.dma_start(on_all[:], io["on_all"].broadcast_to((P, D + ER))).then_inc(late_in, 16)
            sp.dma_start(expert_ids[:], io["c_experts"]).then_inc(late_in, 16)
            for step in steps:
                kind, b = step[0], step[1] if len(step) > 1 else 0
                if kind == "KD":
                    wait_drained(sp, ("LK", b))
                    if b == 0:
                        sp.wait_ge(diag_zeroed, 2)
                        sp.wait_ge(tails_ready, 1)
                    else:
                        wait_full(sp, ("LS", b - 1, NLT - 1))
                    for h in range(H):
                        rows = slice(HD * h, HD * h + HD)
                        sp.dma_start(k_diag[rows, h, :], kT[rows, :]).then_inc(k_diag_in, 16)
                if kind == "MB":
                    side = step[2]
                    sp.wait_ge(split_ready, 2 * b + side + 1)
                    for hp in range(2):
                        for t0, nt, part in STORES[side]:
                            rows = slice(SLOT * hp, SLOT * hp + SLOT)
                            src = parts[rows, side, part:part + nt, :]
                            if side:
                                src = parts[rows, side, part:part + 1, :].broadcast_to((SLOT, nt, S))
                            sp.dma_start(parts_dram[b, side, hp, t0:t0 + nt].rearrange("t p n -> p t n"),
                                         src).then_inc(parts_out, 16)
                if kind == "ST" and b < 2:
                    sp.wait_ge(zeroed, b + 1)
                    for hp in range(2):
                        row = SLOT * hp + SHIFT_ROW
                        sp.dma_start(k_stack[b][row:row + 2, :, :],
                                     rows_dram[0:2, :].rearrange("o (a n) -> o a n", n=S)).then_inc(k_ones_in[b], 16)
                if kind == "ST":
                    sp.wait_ge(parts_out, 16 * 6 * 2 * (b + 1))
                    if b >= 2:
                        wait_full(sp, ("E", b - 2, H // 4 - 1, NT - 1, 0))
                    for side in range(2):
                        for hp in range(2):
                            src = parts_dram[b, side, hp].rearrange("t (d a) n -> (t d) a n", d=HD)
                            rows = slice(SLOT * hp, SLOT * hp + SHIFT_ROW)
                            dst = q_stack[b % 2][rows, :, hp, :] if side else k_stack[b % 2][rows, :, :]
                            sp.dma_start(dst, src).then_inc(stacks_in, 16)
                    for hp in range(2):
                        row = SLOT * hp + SHIFT_ROW
                        sp.dma_start(q_stack[b % 2][row:row + 2, :, hp, :],
                                     rows_dram[2:4, :].rearrange("o (a n) -> o a n", n=S)).then_inc(stacks_in, 16)
                if kind == "SHIFT":
                    wait_drained(sp, step)
                    sp.dma_start(shift_dram[b].rearrange("r p n -> p r n"), shift[:]).then_inc(shift_out, 16)
                    sp.wait_ge(shift_out, 16 * (b + 1))
                    for hp in range(2):
                        row = SLOT * hp + SHIFT_ROW
                        src = shift_dram[b].rearrange("r (e a i) n -> e r a (i n)", e=2, i=NT)[hp]
                        sp.dma_start(q_stack[b % 2][row:row + 2, :, hp, :], src).then_inc(shift_in, 16)
                if kind == "WX":
                    wait_full(sp, ("LS", B - 1, NLT - 1))
                    for n, name in enumerate(("Wg", "Wu", "Wd")):
                        sp.dma_start(w_exp[:, 0, n, :], io[name + "_s"]).then_inc(experts_in, 16)
                        sp.dma_start(w_exp[:, 1:, n, :], io[name + "_r"].rearrange("e p i -> p e i")).then_inc(experts_in, 16)
                if kind == "ADD" and step[2] == NE - 1:
                    sp.wait_ge(added, add_no[step])
                    sp.dma_start(out.rearrange("b (i p) d -> p b i d", p=P)[:, b],
                                 x[:, b * NT:(b + 1) * NT, :]).then_inc(out_done, 16)
            sp.wait_ge(out_done, 16 * B)

        @block.gpsimd
        def _(pool):
            own = [0]

            def link(ins):
                own[0] += 1
                ins.then_inc(g_step, 1)
                pool.wait_ge(g_step, own[0])

            def root(n, batches, rows=2):
                c = slice(batches[0] * NT, (batches[-1] + 1) * NT)
                pool.wait_ge(sqrt_in, n)
                nc.gpsimd.tensor_tensor(nrm[:, 6:6 + rows, c], nrm[:, 4:4 + rows, c], half[:, 0:rows, c],
                                        ALU.pow).then_inc(sqrt_out, 1)
                pool.wait_ge(sqrt_out, n)

            link(nc.gpsimd.memset(half[:], 0.5))
            link(nc.gpsimd.memset(k_diag[:, ACT_CLEARS:, :], 0.0))
            pool.sem_inc(diag_zeroed, 1)
            root(1, range(1))
            nc.gpsimd.memset(pT_loc[:], 0.0).then_inc(pT_cleared, 1)
            pool.wait_ge(pT_cleared, 1)

            def clear(i):
                nc.gpsimd.memset(k_stack[i][:].bitcast(F32), 0.0)
                nc.gpsimd.memset(q_stack[i][:].bitcast(F32), 0.0).then_inc(zeroed, 1)
                pool.wait_ge(zeroed, i + 1)

            clear(0)
            for step in steps:
                if step == ("STATS", 0):
                    root(2, range(1, B))
                if step[0] == "R2":
                    root(step[1] + 3, [step[1]], 1)
                if step == ("MB", 1, 0):
                    clear(1)
                if step[0] == "MB" and step[1] > 0:
                    _, b, side = step
                    n = 2 * b + side + 1
                    pool.wait_ge(rot_ready, n)
                    pool.wait_ge(split_ready, n - 1)
                    if side == 0:
                        pool.wait_ge(parts_out, 16 * 6 * 2 * b)
                    whole = rot[:, side, :]
                    hi, mid, lo = (parts[:, side, t, :] for t in range(3))
                    link(nc.gpsimd.tensor_copy(hi, whole))
                    link(nc.gpsimd.tensor_tensor(rest[:], whole, hi, ALU.subtract))
                    link(nc.gpsimd.tensor_copy(mid, rest[:]))
                    nc.gpsimd.tensor_tensor(lo, rest[:], mid, ALU.subtract).then_inc(split_ready, 1)
                    pool.wait_ge(split_ready, n)

        @block.scalar
        def _(act):
            nc.scalar.memzero(k_diag[:, 0:ACT_CLEARS, :]).then_inc(diag_zeroed, 1)
            act.wait_ge(wide_in, 16)

            def drain(use, dst, src, bias=None, scale=None):
                wait_full(act, use)
                if bias is None and scale is None:
                    ins = nc.scalar.copy(dst, src)
                elif bias is None:
                    ins = nc.scalar.activation(dst, src, ACT.Copy, scale=scale)
                else:
                    ins = nc.scalar.activation(dst, src, ACT.Identity, bias=bias)
                drained_by(ins, use)

            for step in steps:
                kind, b = step[0], step[1] if len(step) > 1 else 0
                bank = bank_of(step) if step in where else None
                if kind == "XT":
                    dst = xrT[:, b, :] if step[2] else xnT[:, b % 2, 0:S]
                    drain(step, dst, bank[:], scale=cols[:, 3:4] if step[2] else None)
                elif kind == "LQ":
                    if b >= 2:
                        wait_full(act, ("LS", b - 2, NLT - 1))
                    drain(step, qT[:, b % 2, 0:S], bank[:], bias=cols[:, 0:1])
                elif kind == "LK":
                    if b:
                        act.wait_ge(k_diag_in, 16 * H * b)
                    drain(step, kT[:, 0:S], bank[:], bias=cols[:, 1:2])
                elif kind == "MV":
                    if b >= 2:
                        act.wait_ge(pv_done, E_PER_B * (b - 1))
                    if b < 2:
                        act.wait_ge(set_up, 3)
                    drain(step, v_mla[:, b % 2, :, :, 0:HD], bank[:].rearrange("p (i h d) -> p i h d", i=NT, h=H))
                elif kind == "MB" and b == 0:
                    side = step[2]
                    act.wait_ge(rot_ready, side + 1)
                    nc.scalar.copy(parts[:, side, 0, :], rot[:, side, :]).then_inc(rounded, 1)
                    act.wait_ge(rest_ready, side + 1)
                    nc.scalar.copy(parts[:, side, 1, :], rest[:]).then_inc(rounded, 1)
                elif kind == "YT":
                    drain(step, yT_mla, bank[:])
                elif kind == "LV":
                    t = NLT * b + step[2]
                    if t < 2:
                        act.wait_ge(set_up, 3)
                    else:
                        wait_full(act, ("LO", (t - 2) // NLT, (t - 2) % NLT))
                    np_ = PAIR * len(LTILES[step[2]])
                    drain(step, v_loc[0:np_, t % 2, :, 0:HD], bank[0:np_, 0:D].rearrange("p (h d) -> p h d", h=H))
                elif kind == "LR":
                    t = NLT * b + step[2]
                    act.wait_ge(loc_turned, t + 1)
                    act.wait_ge(pT_cleared, 1)
                    if t:
                        wait_full(act, ("LO", (t - 1) // NLT, (t - 1) % NLT))
                    for j in range(len(LTILES[step[2]])):
                        rows = slice(PAIR * j, PAIR * j + PAIR)
                        last = nc.scalar.activation(pT_loc[rows, :, rows],
                                                    sT_loc[rows, t % 2, :].rearrange("p (h k) -> p h k", h=H),
                                                    ACT.Exp, scale=SCALE)
                    last.then_inc(loc_exp, 1)
                elif kind == "LO":
                    drain(step, oT_loc[:], bank[:])
                elif kind == "X2T":
                    drain(step, x2T[:, b, :], bank[:], scale=cols[:, 4:5])
                elif kind == "E":
                    _, b, g, j, u = step
                    n, w = pv_no[("PV", b, g, j)], S - j * P
                    heads = exp_units(g, j)[u]
                    if n > P_RING and u == 0:
                        act.wait_ge(pv_done, n - P_RING)
                    wait_full(act, step)
                    src = bank[:, 0:w * len(heads)].rearrange("p (h q) -> p h q", q=w)
                    m = heads[0] - 4 * g
                    drained_by(nc.scalar.activation(p_mla[:, n % P_RING, m:m + len(heads), j * P:], src,
                                                    ACT.Exp, scale=SCALE), step)
                elif kind == "PV" and step[3] == NT - 1:
                    _, b, g, _ = step
                    act.wait_ge(pv_done, pv_no[step])
                    if b and g == 0:
                        wait_full(act, ("X1", b - 1))
                    nc.scalar.copy(oT_mla[:, g, :], bank_c[:]).then_inc(c_drained, 1)
                elif kind == "ROUTE":
                    act.wait_ge(logits_ready, b + 1)
                    nc.scalar.activation(rt[:, 1, :, 0:ER], rt[:, 0, :, 0:ER], ACT.Exp, scale=-1.0).then_inc(logits_exp, 1)
                elif kind == "GU":
                    n = gu_no[step]
                    wait_full(act, step + (0,))
                    if n > 2:
                        act.wait_ge(hid_ready, n - 2)
                    nc.scalar.activation(gate[n % 2], bank_of(step + (0,))[:], ACT.Tanh, scale=0.5).then_inc(gate_ready, 1)

        @block.vector
        def _(dve):
            own = [0]

            def link(ins):
                own[0] += 1
                ins.then_inc(v_step, 1)
                dve.wait_ge(v_step, own[0])

            def begin_statistics(batches):
                ts = range(batches[0] * NT, (batches[-1] + 1) * NT)
                c = slice(ts[0], ts[-1] + 1)
                for t in ts:
                    if t % NT == 0:
                        dve.wait_ge(x_in[t // NT], 16)
                    last = nc.vector.bn_stats(stats[:, t, :], x[:, t, :])
                link(last)
                for t in ts:
                    last = nc.vector.bn_aggr(mv[:, t, :], stats[:, t, :])
                link(last)
                link(nc.vector.tensor_scalar(nrm[:, 4, c], mv[:, c, 1], LN_EPS, None, ALU.add))
                link(nc.vector.reciprocal(nrm[:, 2, c], nrm[:, 4, c]))
                nc.vector.tensor_tensor(nrm[:, 5, c], mv[:, c, 1], nrm[:, 2, c], ALU.mult).then_inc(sqrt_in, 1)

            def end_statistics(batches, n):
                c = slice(batches[0] * NT, (batches[-1] + 1) * NT)
                dve.wait_ge(sqrt_out, n)
                link(nc.vector.reciprocal(nrm[:, 2, c], nrm[:, 6, c]))
                link(nc.vector.tensor_scalar(nrm[:, 1, c], nrm[:, 7, c], RMS_EPS, None, ALU.add))
                link(nc.vector.reciprocal(nrm[:, 3, c], nrm[:, 1, c]))

            link(nc.vector.memset(nrm[:, 4:6, :], 1.0))
            begin_statistics(range(1))
            for bank in banks["M"]:
                nc.vector.memset(bank[:], 0.0)
            nc.vector.memset(bank_c[:], 0.0)
            nc.vector.memset(xnT[:, :, S:], 0.0)
            nc.vector.memset(attnT[:, S:], 0.0).then_inc(set_up, 1)
            nc.vector.memset(v_loc[:, :, :, HD:], 1.0).then_inc(set_up, 1)
            nc.vector.memset(v_mla[:, :, :, :, HD:], 1.0).then_inc(set_up, 1)
            end_statistics(range(1), 1)

            def scratch_read(step):
                before = [s[0] for s in steps[:steps.index(step)]]
                for done, n in ((rot_ready, before.count("MB")), (loc_turned, before.count("LS"))):
                    if n:
                        dve.wait_ge(done, n)

            def outputs(step, dst, np_, den):
                o = bank_of(step)[0:np_, :].rearrange("p (h r) -> p h r", h=H)
                wait_full(dve, step)
                kind, b, i = step
                if i or b:
                    last = ((NLT if kind == "LY" else NT) - 1) if not i else i - 1
                    wait_drained(dve, (kind, b if i else b - 1, last))
                link(nc.vector.reciprocal(den[0:np_, :], o[:, :, HD]))
                drained_by(nc.vector.tensor_tensor(dst.rearrange("p (h d) -> p h d", h=H), o[:, :, 0:HD],
                                                   den[0:np_, :].unsqueeze(2).broadcast_to((np_, H, HD)), ALU.mult), step)

            for step in steps:
                kind, b = step[0], step[1] if len(step) > 1 else 0
                bank = bank_of(step) if step in where else None
                tb = slice(b * NT, (b + 1) * NT)
                if step == ("LK", 0):
                    dve.wait_ge(wide_in, 16)
                    nc.vector.tensor_scalar(kT[:, S:], xnT[:, 0, S:], cols[:, 1:2], None, ALU.add)
                    for n in range(2):
                        last = nc.vector.tensor_scalar(qT[:, n, S:], xnT[:, 0, S:], cols[:, 0:1], None, ALU.add)
                    last.then_inc(tails_ready, 1)
                elif step == ("STATS", 0):
                    begin_statistics(range(1, B))
                elif step == ("STATS", 1):
                    end_statistics(range(1, B), 2)
                elif kind == "WF":
                    wait_full(dve, step)
                    ku, qu, rq = (bank[:, 64 * n:64 * n + 64].rearrange("p (a e d) -> p e d a", e=2, d=HH) for n in range(3))
                    rk = w_ropek.rearrange("p (a e) d -> p e d a", e=2)
                    part = HH // 2
                    nc.vector.memset(w_mla[:, :, 1, :, 0:HH, :], 0.0)
                    for e in range(2):
                        for side, plain, turn in ((0, ku, rk), (1, qu, rq)):
                            nc.vector.tensor_copy(w_mla[:, side, 0, e, 0:HH], plain[:, e])
                            nc.vector.tensor_copy(w_mla[:, side, 0, e, HH:], turn[:, e])
                            nc.vector.tensor_copy(w_mla[:, side, 1, e, HH:HH + part], turn[:, e, part:])
                            nc.vector.tensor_copy(w_mla[:, side, 1, e, HH + part:], turn[:, e, 0:part])
                    drained_by(nc.vector.tensor_copy(w_mla_v[:], bank[:, 192:192 + D]), step)
                elif kind == "LN":
                    for t in range(b * NT, b * NT + NT):
                        last = nc.vector.tensor_scalar(xn[:, t, :], x[:, t, :], mv[:, t, 0:1], nrm[:, 2, t:t + 1],
                                                       ALU.subtract, ALU.mult)
                    last.then_inc(xn_ready, 1)
                    dve.wait_ge(xn_ready, 2 * b + 1)
                    for t in range(b * NT, b * NT + NT):
                        last = nc.vector.tensor_scalar(xr[:, t, :], xn[:, t, :], nrm[:, 3, t:t + 1], None, ALU.mult)
                    last.then_inc(xn_ready, 1)
                elif kind in ("MA", "MB"):
                    side, which = step[2], int(kind == "MB")
                    if b and which == 0:
                        dve.wait_ge(split_ready, 2 * (b - 1) + side + 1)
                    if which:
                        scratch_read(step)
                    dve.wait_ge(rope_in, 16)
                    wait_full(dve, step)
                    dst = turned[:] if which else rot[:, side, :]
                    drained_by(nc.vector.tensor_tensor(dst, bank[:], rope[:, which, :], ALU.mult), step)
                    if which:
                        wait_drained(dve, step)
                        nc.vector.tensor_tensor(rot[:, side, :], rot[:, side, :], turned[:], ALU.add).then_inc(rot_ready, 1)
                    if which and b == 0:
                        if side:
                            dve.wait_ge(split_ready, side)
                        dve.wait_ge(rounded, 2 * side + 1)
                        nc.vector.tensor_tensor(rest[:], rot[:, side, :], parts[:, side, 0, :],
                                                ALU.subtract).then_inc(rest_ready, 1)
                        dve.wait_ge(rounded, 2 * side + 2)
                        dve.wait_ge(rest_ready, side + 1)
                        nc.vector.tensor_tensor(parts[:, side, 2, :], rest[:], parts[:, side, 1, :],
                                                ALU.subtract).then_inc(split_ready, 1)
                elif kind == "S":
                    i, heads = UNITS[step[2]]
                    w = (i + 1) * P
                    wait_full(dve, step)
                    src = bank[:, 0:w * len(heads)].rearrange("p (h k) -> p h k", k=w)
                    if i >= 2:
                        dst = neg_max[:, heads[0] % 2, heads[0] // 2, i:i + 1]
                        n = single.index(step)
                        if n:
                            wait_drained(dve, single[n - 1])
                        drained_by(nc.vector.tensor_tensor_reduce(differences[:, 0:w], masked16[:, S - w:],
                                                                  bank[:, 0:w], -1.0, -NEG, ALU.add, ALU.min, dst), step)
                    else:
                        a0, na = heads[0] // 2, len(heads) // 2
                        dst = neg_max[:, :, a0:a0 + na, i].rearrange("p e a -> p a e")
                        src = src.rearrange("p (a e) k -> p a e k", e=2)
                        drained_by(nc.vector.tensor_reduce(dst, src, AX.X, ALU.max, negate=True), step)
                elif kind == "SHIFT":
                    wait_full(dve, step)
                    if b:
                        dve.wait_ge(shift_out, 16 * b)
                    link(nc.vector.tensor_copy(shift[:, 0, :], bank[0:H * NT, 0:P]))
                    drained_by(nc.vector.tensor_tensor(shift[:, 1, :], bank[0:H * NT, 0:P], shift[:, 0, :],
                                                       ALU.subtract), step)
                elif kind == "LS":
                    t = NLT * b + step[2]
                    np_ = PAIR * len(LTILES[step[2]])
                    sc = bank[0:np_, :].rearrange("p (h k) -> p h k", h=H)
                    wait_full(dve, step)
                    scratch_read(step)
                    link(nc.vector.tensor_reduce(row_max[0:np_, :], sc, AX.X, ALU.max))
                    drained_by(nc.vector.tensor_tensor(s_loc[0:np_, :].rearrange("p (h k) -> p h k", h=H), sc,
                                                       row_max[0:np_, :].unsqueeze(2).broadcast_to((np_, H, PAIR)),
                                                       ALU.subtract), step)
                    wait_drained(dve, step)
                    if t >= 2:
                        dve.wait_ge(loc_exp, t - 1)
                    nc.vector.transpose(sT_loc[0:np_, t % 2, :], s_loc[0:np_, :]).then_inc(loc_turned, 1)
                elif kind == "LY":
                    np_ = PAIR * len(LTILES[step[2]])
                    outputs(step, y_loc[0:np_, :], np_, rden)
                elif kind == "LT":
                    tile = LTILES[step[2]]
                    wait_full(dve, step)
                    if b and step[2] == 0:
                        wait_full(dve, ("LW", b - 1))
                    for n, (g0, ng, first, stp) in enumerate(runs(tile)):
                        dst = attnT[:, tokens(first, stp, PAIR * ng)]
                        src = bank[:, g0 * PAIR:(g0 + ng) * PAIR]
                        if tile[0][0] == "local":
                            last = nc.vector.tensor_scalar(dst, src, cols[:, 2:3], None, ALU.add)
                        else:
                            if step[2] == S // P and n == 0:
                                wait_drained(dve, ("LT", b, S // P - 1))
                            last = nc.vector.scalar_tensor_tensor(out=dst, in0=src, scalar=cols[:, 2:3], in1=dst,
                                                                  op0=ALU.add, op1=ALU.add)
                    drained_by(last, step)
                elif kind == "LW":
                    dve.wait_ge(late_in, 16 * 2)
                    wait_full(dve, step)
                    for t in range(b * NT, b * NT + NT):
                        last = nc.vector.tensor_tensor(x[:, t, :], x[:, t, :], bo_all, ALU.add)
                    link(last)
                    drained_by(nc.vector.tensor_tensor(x[:, tb, :], bank[:].rearrange("p (i d) -> p i d", i=NT),
                                                       x[:, tb, :], ALU.add), step)
                elif kind == "Y":
                    outputs(step, y_mla[:, step[2], :], P, rden_mla)
                elif kind == "X1":
                    wait_full(dve, step)
                    drained_by(nc.vector.tensor_tensor(x1[:, tb, :], bank[:].rearrange("p (i d) -> p i d", i=NT),
                                                       xn[:, tb, :], ALU.add), step)
                elif kind == "R2":
                    wait_drained(dve, ("X1", b))
                    for t in range(b * NT, b * NT + NT):
                        last = nc.vector.tensor_tensor_reduce(xn[:, t, :], x1[:, t, :], x1[:, t, :], 1.0 / D, 0.0,
                                                              ALU.mult, ALU.add, nrm[:, 4, t:t + 1])
                    last.then_inc(sqrt_in, 1)
                    wait_drained(dve, ("LW", b))
                    nc.vector.tensor_tensor(x[:, tb, :], x[:, tb, :], x1[:, tb, :], ALU.add)
                elif kind == "R3":
                    dve.wait_ge(sqrt_out, b + 3)
                    link(nc.vector.tensor_scalar(nrm[:, 1, tb], nrm[:, 6, tb], RMS_EPS, None, ALU.add))
                    link(nc.vector.reciprocal(nrm[:, 2, tb], nrm[:, 1, tb]))
                    for t in range(b * NT, b * NT + NT):
                        last = nc.vector.tensor_scalar(xn[:, t, :], x1[:, t, :], nrm[:, 2, t:t + 1], None, ALU.mult)
                    last.then_inc(x2_ready, 1)
                elif kind == "ROUTE":
                    wait_full(dve, step)
                    drained_by(nc.vector.tensor_tensor(rt[:, 0, :, 0:ER],
                                                       bank[:, 0:NT * ER].rearrange("p (t e) -> p t e", e=ER),
                                                       router_bias.unsqueeze(1).broadcast_to((P, NT, ER)), ALU.add), step)
                    wait_drained(dve, step)
                    nc.vector.memset(rt[:, 3, :, ER:], -1.0).then_inc(logits_ready, 1)
                elif kind == "PICK":
                    dve.wait_ge(logits_exp, b + 1)
                    link(nc.vector.tensor_scalar(rt[:, 1, :, 0:ER], rt[:, 1, :, 0:ER], 1.0, None, ALU.add))
                    link(nc.vector.reciprocal(rt[:, 3, :, 0:ER], rt[:, 1, :, 0:ER]))
                    for t in range(NT):
                        last = nc.vector.max(rt[:, 2, t, :], rt[:, 3, t, :])
                    link(last)
                    for t in range(NT):
                        last = nc.vector.max_index(rt_idx[:, t, :], rt[:, 2, t, :], rt[:, 3, t, :])
                    link(last)
                    link(nc.vector.tensor_copy(rt[:, 0, :, :], rt_idx[:]))
                    link(nc.vector.tensor_tensor(rt_sum[:, 0, :], rt[:, 2, :, 0], rt[:, 2, :, 1], ALU.add))
                    link(nc.vector.reciprocal(rt_sum[:, 1, :], rt_sum[:, 0, :]))
                    link(nc.vector.tensor_scalar(rt_sum[:, 1, :], rt_sum[:, 1, :], 0.5, None, ALU.mult))
                    link(nc.vector.tensor_tensor(rt[:, 2, :, 0:2], rt[:, 2, :, 0:2],
                                                 rt_sum[:, 1, :].unsqueeze(2).broadcast_to((P, NT, 2)), ALU.mult))
                    for n in range(2):
                        link(nc.vector.tensor_tensor(rt[:, 4 + n, :, :], rt[:, 0, :, n:n + 1].broadcast_to((P, NT, 8)),
                                                     expert_ids[:].unsqueeze(1).broadcast_to((P, NT, 8)), ALU.is_equal))
                        link(nc.vector.tensor_tensor(rt[:, 4 + n, :, :], rt[:, 4 + n, :, :],
                                                     rt[:, 2, :, n:n + 1].broadcast_to((P, NT, 8)), ALU.mult))
                    link(nc.vector.tensor_tensor(expert_w[:, tb, :], rt[:, 4, :, :], rt[:, 5, :, :], ALU.add))
                elif kind == "GU":
                    n = gu_no[step]
                    dve.wait_ge(gate_ready, n)
                    if n > 2:
                        wait_full(dve, downs[n - 3])
                    drained_by(nc.vector.scalar_tensor_tensor(out=hid[n % 2], in0=gate[n % 2], scalar=1.0,
                                                              in1=bank_of(step + (0,))[:], op0=ALU.add, op1=ALU.mult),
                               step + (0,))
                    wait_drained(dve, step + (0,))
                    wait_full(dve, step + (1,))
                    ins = nc.vector.tensor_tensor(hid[n % 2], bank_of(step + (1,))[:], hid[n % 2], ALU.mult)
                    drained_by(ins, step + (1,))
                    wait_drained(dve, step + (1,))
                    dve.sem_inc(hid_ready, 1)
                elif kind == "ADD":
                    _, c, e = step
                    down_use = ("DOWN", c, e)
                    wait_full(dve, down_use)
                    down = bank_of(down_use)[:].rearrange("p (i d) -> p i d", i=NT)
                    if add_no[step] > 1:
                        dve.wait_ge(added, add_no[step] - 1)
                    for i in range(NT):
                        t = c * NT + i
                        weight = 0.5 if e == 0 else expert_w[:, t, e - 1:e]
                        ins = nc.vector.scalar_tensor_tensor(out=x[:, t, :], in0=down[:, i, :], scalar=weight,
                                                             in1=x[:, t, :], op0=ALU.mult, op1=ALU.add)
                    drained_by(ins, down_use)
                    wait_drained(dve, down_use)
                    dve.sem_inc(added, 1)

        @block.tensor
        def _(pe):
            pe.wait_ge(set_up, 3)
            pe.wait_ge(eye_in, 16)
            for step in steps:
                kind, b = step[0], step[1] if len(step) > 1 else 0
                if step in where and kind != "SHIFT":
                    wait_free(pe, step)
                    bank = bank_of(step)
                if kind == "WF":
                    pe.wait_ge(lat_in, 16)
                    for down, c0, c1 in ((0, 0, 64), (1, 64, 128), (1, 128, 192), (0, 192, 192 + D)):
                        last = nc.tensor.matmul(bank[:, c0:c1], w_down_lat[:, down, :], w_up_lat[:, c0:c1],
                                                start=True, stop=True)
                    full_by(last, step)
                elif kind in ("XT", "X2T"):
                    second = kind == "X2T"
                    if second:
                        pe.wait_ge(x2_ready, b + 1)
                    else:
                        pe.wait_ge(xn_ready, 2 * b + 1 + step[2])
                    src = xr if not second and step[2] else xn
                    for i in range(NT):
                        last = nc.tensor.transpose(bank[:, i * P:(i + 1) * P], src[:, b * NT + i, :], eye[:])
                    full_by(last, step)
                elif kind in ("LQ", "LK"):
                    pe.wait_ge(wide_in, 16)
                    wait_drained(pe, ("XT", b, 0))
                    full_by(nc.tensor.matmul(bank[:], w_attn[:, int(kind == "LK"), :], xnT[:, b % 2, 0:S], start=True,
                                             stop=True), step)
                elif kind in ("MA", "MB"):
                    wait_drained(pe, ("WF",))
                    wait_drained(pe, ("XT", b, 1))
                    full_by(nc.tensor.matmul(bank[:], w_mla[:, step[2], int(kind == "MB")].rearrange("p e d a -> p (e d a)"), xrT[:, b, :], start=True,
                                             stop=True), step)
                elif kind == "MV":
                    for i in range(NT):
                        last = nc.tensor.matmul(bank[:, i * D:(i + 1) * D], xrT[:, b, i * P:(i + 1) * P], w_mla_v[:],
                                                start=True, stop=True)
                    full_by(last, step)
                elif kind == "S":
                    i, heads = UNITS[step[2]]
                    w = (i + 1) * P
                    if step[2] == 0:
                        pe.wait_ge(k_ones_in[b % 2], 16 * 2)
                        pe.wait_ge(stacks_in, STACK_IN * (b + 1))
                    for n, h in enumerate(heads):
                        last = nc.tensor.matmul(bank[:, n * w:(n + 1) * w],
                                                q_stack[b % 2][:, h // 2, h % 2, i * P:(i + 1) * P],
                                                k_stack[b % 2][:, h // 2, 0:w], start=True, stop=i >= 2,
                                                skip_group_check=True)
                        if i < 2:
                            last = nc.tensor.matmul(bank[:, (n + 1) * w - P:(n + 1) * w], eye16, causal16,
                                                    start=False, stop=True, skip_group_check=True)
                    full_by(last, step)
                elif kind == "SHIFT":
                    wait_drained(pe, ("S", b, len(UNITS) - 1))
                    wait_free(pe, step)
                    full_by(nc.tensor.transpose(bank_of(step)[0:H * NT, 0:P], neg_max[:].rearrange("p e a i -> p (e a i)"),
                                                eye[:]), step)
                elif kind == "E":
                    _, b, g, j, u = step
                    w = S - j * P
                    if step[2:] == (0, 0, 0):
                        pe.wait_ge(shift_in, 32 * (b + 1))
                    for m, h in enumerate(exp_units(g, j)[u]):
                        nc.tensor.matmul(bank[:, m * w:(m + 1) * w], k_stack[b % 2][:, h // 2, j * P:(j + 1) * P],
                                         q_stack[b % 2][:, h // 2, h % 2, j * P:], start=True, stop=False,
                                         skip_group_check=True)
                        last = nc.tensor.matmul(bank[:, m * w:m * w + P], eye16, causalT16,
                                                start=False, stop=True, skip_group_check=True)
                    full_by(last, step)
                elif kind == "PV":
                    _, b, g, j = step
                    n = pv_no[step]
                    wait_drained(pe, ("E", b, g, j, len(exp_units(g, j)) - 1))
                    wait_drained(pe, ("MV", b))
                    if j == 0 and n > 1:
                        pe.wait_ge(c_drained, (n - 1) // NT)
                    for m in range(4):
                        last = nc.tensor.matmul(bank_c[32 * m:32 * m + HD + 1, j * P:], v_mla[:, b % 2, j, 4 * g + m, :],
                                                p_mla[:, n % P_RING, m, j * P:], start=(j == 0), stop=(j == NT - 1),
                                                skip_group_check=True)
                    last.then_inc(pv_done, 1)
                elif kind == "Y":
                    if step[2] == 0:
                        pe.wait_ge(c_drained, (b + 1) * (H // 4))
                    for g in range(4):
                        last = nc.tensor.transpose(bank[:, g * P:(g + 1) * P], oT_mla[:, g, step[2] * P:(step[2] + 1) * P],
                                                   eye[:])
                    full_by(last, step)
                elif kind == "YT":
                    wait_drained(pe, ("Y", b, NT - 1))
                    for i in range(NT):
                        last = nc.tensor.transpose(bank[:, i * P:(i + 1) * P], y_mla[:, i, :], eye[:])
                    full_by(last, step)
                elif kind == "X1":
                    wait_drained(pe, ("YT", b))
                    for i in range(NT):
                        last = nc.tensor.matmul(bank[:, i * D:(i + 1) * D], yT_mla[:, i * P:(i + 1) * P], w_mla_o,
                                                start=True, stop=True)
                    full_by(last, step)
                elif kind == "LV":
                    for j, (_, first, stp) in enumerate(LTILES[step[2]]):
                        last = nc.tensor.matmul(bank[PAIR * j:PAIR * j + PAIR, 0:D], xnT[:, b % 2, tokens(first, stp)],
                                                w_attn[:, 2, :], start=True, stop=True, skip_group_check=True)
                    full_by(last, step)
                elif kind == "LS":
                    if step[2] == 0:
                        pe.wait_ge(k_diag_in, 16 * H * (b + 1))
                        wait_drained(pe, ("LQ", b))
                        if b == 0:
                            pe.wait_ge(masks_in, 16)
                            pe.wait_ge(tails_ready, 1)
                    np_ = PAIR * len(LTILES[step[2]])
                    nc.tensor.matmul(bank[0:np_, :], eye16[:, 0:np_], pair16, start=True, stop=False, skip_group_check=True)
                    for j, (_, first, stp) in enumerate(LTILES[step[2]]):
                        last = nc.tensor.matmul(bank[PAIR * j:PAIR * j + PAIR, :], qT[:, b % 2, tokens(first, stp)],
                                                k_diag[:, :, tokens(first, stp)], start=False, stop=True,
                                                skip_group_check=True)
                    full_by(last, step)
                elif kind == "LO":
                    t = NLT * b + step[2]
                    np_ = PAIR * len(LTILES[step[2]])
                    pe.wait_ge(loc_exp, t + 1)
                    wait_drained(pe, ("LV", b, step[2]))
                    for h in range(H):
                        m, c = h % 4, h // 4 * P
                        last = nc.tensor.matmul(bank[32 * m:32 * m + HD + 1, c:c + np_], v_loc[0:np_, t % 2, h, :],
                                                pT_loc[0:np_, h, 0:np_], start=True, stop=True, skip_group_check=True)
                    full_by(last, step)
                elif kind == "LY":
                    np_ = PAIR * len(LTILES[step[2]])
                    wait_drained(pe, ("LO", b, step[2]))
                    for g in range(4):
                        last = nc.tensor.transpose(bank[0:np_, g * P:(g + 1) * P], oT_loc[:, g * P:g * P + np_], eye[:])
                    full_by(last, step)
                elif kind == "LT":
                    np_ = PAIR * len(LTILES[step[2]])
                    wait_drained(pe, ("LY", b, step[2]))
                    full_by(nc.tensor.transpose(bank[:, 0:np_], y_loc[0:np_, :], eye[0:np_, 0:np_]), step)
                elif kind == "LW":
                    wait_drained(pe, ("LT", b, NLT - 1))
                    for i in range(NT):
                        last = nc.tensor.matmul(bank[:, i * D:(i + 1) * D], attnT[:, i * P:(i + 1) * P], w_attn[:, 3, :],
                                                start=True, stop=True)
                    full_by(last, step)
                elif kind == "ROUTE":
                    wait_drained(pe, ("X2T", b))
                    for i in range(NT):
                        last = nc.tensor.matmul(bank[:, i * ER:(i + 1) * ER], x2T[:, b, i * P:(i + 1) * P],
                                                w_router, start=True, stop=True)
                    full_by(last, step)
                elif kind == "GU":
                    _, c, e = step
                    if e == 0:
                        wait_drained(pe, ("X2T", c))
                        pe.wait_ge(experts_in, 16 * 6)
                    for m in range(2):
                        use = step + (m,)
                        wait_free(pe, use)
                        full_by(nc.tensor.matmul(bank_of(use)[:], w_exp[:, e, m, :], x2T[:, c, :], start=True, stop=True), use)
                elif kind == "DOWN":
                    _, c, e = step
                    n = gu_no[("GU", c, e)]
                    pe.wait_ge(hid_ready, n)
                    for i in range(NT):
                        last = nc.tensor.matmul(bank[:, i * D:(i + 1) * D], hid[n % 2][:, i * P:(i + 1) * P],
                                                w_exp[:, e, 2, :], start=True, stop=True)
                    full_by(last, step)


_TURNED = ("Wq", "Wk", "Wv", "Wo", "W_kvd", "W_qd")
_NAMES = ["L0_attn_" + n for n in ("x", "Wq", "bq", "Wk", "bk", "Wv", "bv", "Wo", "bo")] + ["L0_ffn_" + n for n in (
    "w_ln1", "w_ln2", "W_kvd", "W_qd", "W_ku", "W_qu", "W_vu", "W_ropeq", "W_ropek", "W_o", "Wg_s", "Wu_s", "Wd_s",
    "Wg_r", "Wu_r", "Wd_r", "W_router", "routing_bias")]


def kernel(**inputs):
    import numpy as _np
    import concourse.bacc as _bacc
    from concourse import mybir as _mybir
    from concourse.bass_utils import run_bass_kernel_spmd as _run

    nc = _bacc.Bacc("TRN2", target_bir_lowering=False, num_devices=1)
    laid = {}
    for full in _NAMES:
        name = full.split("_", 2)[2]
        a = _np.asarray(inputs[full])
        laid[name] = _np.ascontiguousarray(a.T if name in _TURNED else a)
    laid["wide"] = _np.concatenate([laid.pop(n).reshape(P, -1) for n in WIDE], axis=1)
    laid["lat"] = _np.concatenate([laid.pop(n) for n in LATS], axis=1)
    laid["on_all"] = _np.concatenate([laid.pop(n) for n in ("bo", "routing_bias")])[None]
    laid.update(constants())
    arrays, io = {}, {}
    for name, a in laid.items():
        arrays[f"in_{name}"] = a
        io[name] = nc.dram_tensor(f"in_{name}", a.shape, _mybir.dt.from_np(a.dtype), kind="ExternalInput").ap()
    out = nc.dram_tensor("out_0", (B, S, D), _mybir.dt.float32, kind="ExternalOutput").ap()
    build(nc, io, out)
    r = _run(nc, [arrays], core_ids=[0])
    return r.results[0]["out_0"]
```

```python
from contextlib import ExitStack

import numpy as np

import concourse.bass as bass
from concourse import mybir

F32 = mybir.dt.float32
BF16 = mybir.dt.bfloat16
U32 = mybir.dt.uint32
ALU = mybir.AluOpType
ACT = mybir.ActivationFunctionType
AX = mybir.AxisListType

P = 128
B = 4
S = 512
D = 128
H = 16
HD = 8
HH = HD // 2
LAT = D // 4
NT = S // P
TILES = B * NT
CHUNK = 16
DIL = 3
PAIR = 2 * CHUNK
LPH = -(-S // DIL)
LPH_PAIRS = -(-LPH // PAIR)
SX = LPH_PAIRS * PAIR * DIL
ER = 7
NE = ER + 1
LN_EPS = 1e-5
RMS_EPS = 1e-5
SCALE = float(HD) ** -0.5
NEG = -1e30
TERMS = 6
STORES = (((0, 3, 0), (3, 2, 0), (5, 1, 0)),
          ((0, 3, 0), (3, 2, 1), (5, 1, 2)))
SLOT = 64
SHIFT_ROW = TERMS * HD
P_RING = 2


def columns(widths):
    at, found = 0, {}
    for name, width in widths:
        found[name] = slice(at, at + width)
        at += width
    return found, at


WIDE, WIDE_END = columns([(n, D) for n in ("Wq", "Wk", "Wv", "Wo")] + [("W_ropek", H * HH), ("W_o", D), ("W_router", ER)]
                         + [(n, 1) for n in ("bq", "bk", "bv", "w_ln1", "w_ln2")])
LATS, LAT_END = columns([("W_kvd", D), ("W_qd", D), ("W_ku", H * HH), ("W_qu", H * HH), ("W_ropeq", H * HH),
                         ("W_vu", D)])
BANKS = {"A": 2, "B": 3, "M": 2}

GROUPS = [[("local", g * PAIR, 1) for g in range(S // PAIR)],
          [("dilated", r + DIL * PAIR * g, DIL) for r in range(DIL) for g in range(LPH_PAIRS)]]
LTILES = [gs[n:n + 4] for gs in GROUPS for n in range(0, len(gs), 4)]
NLT = len(LTILES)
LOCAL_TILES = S // P


def score_units():
    units = []
    for g in range(H // 4):
        for i in range(NT):
            n = S // ((i + 1) * P)
            units += [(i, list(range(h, min(h + n, 4 * g + 4)))) for h in range(4 * g, 4 * g + 4, n)]
    return units


UNITS = score_units()
PER_GROUP = len(UNITS) // (H // 4)


def exp_units(g, j):
    n = max(1, 512 // (S - j * P))
    return [list(range(h, h + n)) for h in range(4 * g, 4 * g + 4, n)]


SPREAD = {
    "latent": [(0, 1.12), (1.12, 2.02), (2.02, 2.86), (2.86, 4)],
    "maxima": [(-0.29, 0.63), (0.61, 1.44), (1.56, 2.46), (2.49, 3.54)],
    "local": [(-0.53, 0.39), (0.36, 1.22), (1.34, 2.21), (2.28, 3.15)],
    "project": [(0.01, 0.29), (0.35, 1.13), (1.49, 2.32)],
    "stacks": [(-0.37, -0.37), (0.48, 0.48), (1.3, 1.3), (2.29, 2.29)],
    "values": [(-1.27, -1.27), (0.38, 0.38), (1.36, 1.36), (2.34, 2.34)],
    "outputs": [(1.18, 1.34), (2.12, 2.26), (2.86, 2.97), (4.02, 4.27)],
    "norm": [(1.31, 1.53), (2.33, 2.54), (3.17, 3.65), (4.28, 4.57)],
    "experts": [(3.17, 5.49)],
    "statistics": [(-0.41, -0.41)],
}


def merged(*parts):
    keyed = [(lo + (hi - lo) * (k + 0.5) / len(one), n, k, step)
             for n, (one, lo, hi) in enumerate(parts) for k, step in enumerate(one)]
    return [x[3] for x in sorted(keyed, key=lambda x: x[:3])]


def plan():
    def project(b):
        return [("LN", b), ("XT", b, 0), ("LK", b), ("LQ", b), ("XT", b, 1), ("MA", b, 0), ("MB", b, 0),
                ("MA", b, 1), ("MB", b, 1)]

    def maxima(b):
        steps = []
        for g in range(H // 4):
            steps += [("S", b, u) for u in range(PER_GROUP * g, PER_GROUP * g + PER_GROUP)] + [("SHIFT", b, g)]
        return steps

    def latent(b):
        steps, late = [], []
        for g in range(H // 4):
            for j in range(NT):
                units = [("E", b, g, j, u) for u in range(len(exp_units(g, j)))]
                steps += units[:1] + late + units[1:]
                late = [("PV", b, g, j)]
        return steps + late

    def outputs(b):
        return [("Y", b, i) for i in range(NT)] + [("YT", b), ("X1", b)]

    def norm(b):
        return [("R2", b), ("R3", b), ("X2T", b), ("ROUTE", b), ("PICK", b)]

    def local(b):
        stages = [("LT", 4), ("LY", 3), ("LO", 2), ("LR", 1), ("LV", 1), ("LS", 0)]
        steps = []
        for k in range(NLT + 4):
            steps += [(stage, b, k - later) for stage, later in stages if 0 <= k - later < NLT]
            if k == NLT - 1:
                steps.append(("KD", b + 1) if b + 1 < B else ("WX",))
        return steps + [("LW", b)]

    def experts(batches):
        moe = [(c, e) for c in batches for e in range(NE)]
        steps = []
        for n in range(len(moe) + 1):
            if n < len(moe):
                steps.append(("GU",) + moe[n])
            if n:
                steps.append(("DOWN",) + moe[n - 1])
        return steps

    first = project(0)
    steps = first[:4] + [("KD", 0), ("WF",)] + first[4:]
    at = SPREAD
    lists = [(experts(range(B)), *at["experts"][0])]
    for b in range(B):
        lists += [(latent(b), *at["latent"][b]), (maxima(b), *at["maxima"][b]), (local(b), *at["local"][b]),
                  (outputs(b), *at["outputs"][b]), (norm(b), *at["norm"][b]), ([("ST", b)], *at["stacks"][b]),
                  ([("MV", b)], *at["values"][b])]
    for b in range(1, B):
        lists.append(([("STATS", 1)] * (b == 1) + project(b), *at["project"][b - 1]))
    lists.append(([("STATS", 0)], *at["statistics"][0]))
    return steps + merged(*lists)


def bank_uses(step):
    kind = step[0]
    if kind in ("S", "LS", "DOWN"):
        return [("A", step)]
    if kind == "E":
        return [("B", step)]
    if kind == "GU":
        return [("B", step + (m,)) for m in range(2)]
    if kind in ("WF", "XT", "LQ", "LK", "MA", "MB", "MV", "SHIFT", "Y", "YT", "X1", "LV", "LO", "LY", "LT", "LW",
                "X2T", "ROUTE"):
        return [("M", step)]
    return []


class Ring:

    def __init__(self, steps, name):
        uses = [use for step in steps for ring, use in bank_uses(step) if ring == name]
        self.bank = {use: n % BANKS[name] for n, use in enumerate(uses)}
        self.count = {use: n // BANKS[name] + 1 for n, use in enumerate(uses)}


def numbers(steps, kinds):
    return {s: n + 1 for n, s in enumerate([s for s in steps if s[0] in kinds])}


def as_bf16(a):
    bits = np.ascontiguousarray(a, np.float32).view(np.uint32).astype(np.uint64)
    return ((bits + 0x7FFF + ((bits >> 16) & 1)) >> 16).astype(np.uint16)


def constants():
    eye = np.eye(P, dtype=np.float32)
    q, k = np.arange(P)[:, None], np.arange(P)[None, :]
    causal = np.where(k > q, NEG, 0.0).astype(np.float32)
    row_chunk = (np.arange(P)[:, None] // CHUNK) % 2
    col_chunk = (np.arange(H * PAIR)[None, :] // CHUNK) % 2
    pair = np.where(row_chunk != col_chunk, NEG, 0.0).astype(np.float32)
    inv = 1.0 / np.float32(10000.0) ** (np.arange(0, HH, 2, dtype=np.float32) / np.float32(HH))
    freqs = np.outer(np.arange(S, dtype=np.float32), inv.astype(np.float32))
    emb = np.concatenate([freqs, freqs], axis=-1)
    cos, sin = np.cos(emb).astype(np.float32), np.sin(emb).astype(np.float32)
    sin[:, :HH // 2] *= -1
    cosT = np.concatenate([np.ones((HH, S), np.float32), cos.T])
    sinT = np.concatenate([np.zeros((HH, S), np.float32), sin.T])
    return {
        "c_eye": eye,
        "c_masks": as_bf16(np.concatenate([eye, causal, causal.T, pair, np.zeros((P, S - P), np.float32), causal],
                                          axis=1)),
        "c_rope": np.stack([np.tile(np.repeat(t, H // 2, axis=0), (2, 1)) for t in (cosT, sinT)], axis=1),
        "c_rows": as_bf16(np.repeat([[1.0], [1.0], [0.0], [0.0]], H // 2 * S, axis=1)),
        "c_experts": np.broadcast_to(np.arange(8, dtype=np.float32), (P, 8)).copy(),
    }


def build(nc, io, out):
    steps = plan()
    rings = {name: Ring(steps, name) for name in BANKS}
    where = {use: (ring, rings[ring].bank[use], rings[ring].count[use])
             for step in steps for ring, use in bank_uses(step)}
    pv_no = numbers(steps, {"PV"})
    gu_no, down_no = numbers(steps, {"GU"}), numbers(steps, {"DOWN"})
    single = [step for step in steps if step[0] == "S" and UNITS[step[2]][0] >= 2]
    downs = [step for step in steps if step[0] == "DOWN"]

    with ExitStack() as ctx:
        def sb(name, shape, dt=F32):
            return ctx.enter_context(nc.sbuf_tensor(name, shape, dt))

        def psum(name, shape):
            return ctx.enter_context(nc.psum_tensor(name, shape, F32))

        def sem(name):
            return ctx.enter_context(nc.semaphore(name))

        banks = {name: [psum(f"bank_{name}{i}", [P, 512]) for i in range(n)] for name, n in BANKS.items()}
        bank_c = psum("bank_c", [P, 512])

        eye = sb("eye", [P, P])
        masks = sb("masks", [P, 3 * P + 512 + S], BF16)
        eye16, causal16, causalT16, pair16 = (masks[:, 0:P], masks[:, P:2 * P], masks[:, 2 * P:3 * P],
                                              masks[:, 3 * P:3 * P + 512])
        masked16 = masks[:, 3 * P + 512:]
        rope = sb("rope", [P, 2, S])
        expert_ids = sb("expert_ids", [P, 8])
        wide = sb("wide", [P, WIDE_END])
        w_attn = wide[:, 0:4 * D].rearrange("p (n d) -> p n d", n=4)
        w_ropek = wide[:, WIDE["W_ropek"]].rearrange("p (h d) -> p h d", h=H)
        w_mla_o = wide[:, WIDE["W_o"]]
        w_router = wide[:, WIDE["W_router"]]
        cols = wide[:, WIDE["bq"].start:WIDE["w_ln2"].stop]
        lat_room = sb("lat_room", [P, LAT_END])
        lat = lat_room[0:LAT, :]
        w_down_lat = lat[:, 0:2 * D].rearrange("p (n d) -> p n d", n=2)
        w_up_lat = lat[:, 2 * D:]
        w_mla = sb("w_mla", [P, 2, 2, 2, HD, H // 2])
        w_mla_v = sb("w_mla_v", [P, D])
        on_all = sb("on_all", [P, D + ER])
        bo_all, router_bias = on_all[:, 0:D], on_all[:, D:]
        x = sb("x", [P, TILES, D])
        xn = sb("xn", [P, TILES, D])
        x1 = sb("x1", [P, TILES, D])
        xr = x1
        xnT = sb("xnT", [P, 2, SX])
        xrT = sb("xrT", [P, B, S])
        x2T = xrT
        stats = sb("stats", [P, TILES, 6])
        mv = sb("mv", [P, TILES, 2])
        nrm = sb("nrm", [P, 8, TILES])
        half = sb("half", [P, 2, TILES])
        qT = sb("qT", [P, 2, SX])
        kT = sb("kT", [P, SX])
        k_diag = sb("k_diag", [P, H, SX])
        v_loc = sb("v_loc", [P, 2, H, HD + 1])
        scratch = sb("scratch", [P, 512])
        s_loc = scratch
        sT_loc = sb("sT_loc", [P, 2, 512])
        pT_loc = sb("pT_loc", [P, H, P])
        row_max = sb("row_max", [P, H])
        oT_loc = sb("oT_loc", [P, 512])
        y_loc = sb("y_loc", [P, D])
        rden = sb("rden", [P, H])
        attnT = sb("attnT", [P, SX])
        rot = sb("rot", [P, 2, S])
        turned = scratch
        parts = sb("parts", [P, 2, 3, S], BF16)
        rest = sb("rest", [P, S])
        k_stack = [sb(f"k_stack{i}", [P, H // 2, S], BF16) for i in range(2)]
        q_stack = [sb(f"q_stack{i}", [P, H // 2, 2, S], BF16) for i in range(2)]
        differences = sb("differences", [P, S], BF16)
        neg_max = sb("neg_max", [P, H // 4, 2, 2, NT])
        shift = sb("shift", [4 * NT, 2, P], BF16)
        v_mla = sb("v_mla", [P, 2, NT, H, HD + 1])
        p_mla = sb("p_mla", [P, P_RING, 4, S])
        oT_mla = sb("oT_mla", [P, 4, S])
        y_mla = lat_room[:, 0:NT * D].rearrange("p (i d) -> p i d", i=NT)
        yT_mla = oT_mla[:, 0, :]
        rden_mla = sb("rden_mla", [P, H])
        late = k_diag[:].rearrange("p h n -> p (h n)")
        w_exp = late[:, 0:NE * 3 * D].rearrange("p (e n d) -> p e n d", e=NE, n=3)
        GATE0 = NE * 3 * D
        gate = [late[:, GATE0 + S * n:GATE0 + S * n + S] for n in range(2)]
        hid = [late[:, GATE0 + S * (n + 2):GATE0 + S * (n + 3)] for n in range(2)]
        rt = sb("rt", [P, 6, NT, 8])
        rt_idx = sb("rt_idx", [P, NT, 8], U32)
        rt_sum = sb("rt_sum", [P, 2, NT])
        expert_w = sb("expert_w", [P, TILES, 8])

        parts_dram = nc.dram_tensor("parts_dram", [B, 2, 2, TERMS, HD * H // 2, S], BF16, kind="Internal").ap()
        shift_dram = nc.dram_tensor("shift_dram", [B, H // 4, 2, 4 * NT, P], BF16, kind="Internal").ap()
        rows_dram = io["c_rows"].bitcast(BF16)

        x_in = [sem(f"x_in{b}") for b in range(B)]
        eye_in, masks_in, rope_in = sem("eye_in"), sem("masks_in"), sem("rope_in")
        wide_in, lat_in = sem("wide_in"), sem("lat_in")
        late_in = sem("late_in")
        experts_in = sem("experts_in")
        k_ones_in = [sem(f"k_ones_in{i}") for i in range(2)]
        k_diag_in = sem("k_diag_in")
        parts_out = sem("parts_out")
        stacks_in = sem("stacks_in")
        shift_out = sem("shift_out")
        shift_in = [sem(f"shift_in{g}") for g in range(H // 4)]
        out_done = sem("out_done")
        set_up = sem("set_up")
        ones_set = sem("ones_set")
        pT_cleared = sem("pT_cleared")
        zeroed = sem("zeroed")
        diag_zeroed = sem("diag_zeroed")
        xn_ready, xr_ready = sem("xn_ready"), sem("xr_ready")
        bias_added = sem("bias_added")
        summed = sem("summed")
        x2_ready = sem("x2_ready")
        sqrt_in, sqrt_out = sem("sqrt_in"), sem("sqrt_out")
        full = {name: [sem(f"full_{name}{i}") for i in range(n)] for name, n in BANKS.items()}
        drained = {name: [sem(f"drained_{name}{i}") for i in range(n)] for name, n in BANKS.items()}
        pv_done, c_drained = sem("pv_done"), sem("c_drained")
        loc_turned = sem("loc_turned")
        loc_exp = sem("loc_exp")
        rot_ready = sem("rot_ready")
        rounded, rest_ready = sem("rounded"), sem("rest_ready")
        split_ready = sem("split_ready")
        gate_ready = sem("gate_ready")
        hid_ready = sem("hid_ready")
        added = sem("added")
        logits_ready, logits_exp = sem("logits_ready"), sem("logits_exp")
        tails_ready = sem("tails_ready")
        v_step, g_step = sem("v_step"), sem("g_step")

        def tokens(first, step, n=PAIR):
            return slice(first, first + step * (n - 1) + 1, step)

        def runs(tile):
            found = []
            for n, (_, first, step) in enumerate(tile):
                if found and found[-1][2] + found[-1][1] * PAIR * step == first:
                    found[-1][1] += 1
                else:
                    found.append([n, 1, first, step])
            return found

        def bank_of(use):
            ring, i, _ = where[use]
            return banks[ring][i]

        def wait_full(eng, use):
            ring, i, n = where[use]
            eng.wait_ge(full[ring][i], n)

        def wait_drained(eng, use):
            ring, i, n = where[use]
            eng.wait_ge(drained[ring][i], n)

        def wait_free(eng, use):
            ring, i, n = where[use]
            if n > 1:
                eng.wait_ge(drained[ring][i], n - 1)

        def full_by(ins, use):
            ins.then_inc(full[where[use][0]][where[use][1]], 1)

        def drained_by(ins, use):
            ins.then_inc(drained[where[use][0]][where[use][1]], 1)

        PV_PER_B = NT * (H // 4)
        STACK_IN = 16 * 6
        ACT_CLEARS = 12

        block = ctx.enter_context(nc.Block())

        @block.sync
        def _(sp):
            xv = io["x"].rearrange("b (i p) d -> p b i d", p=P)
            def load_x(b):
                sp.dma_start(x[:, b * NT:(b + 1) * NT, :], xv[:, b]).then_inc(x_in[b], 16)

            load_x(0)
            sp.dma_start(eye[:], io["c_eye"]).then_inc(eye_in, 16)
            sp.dma_start(wide[:], io["wide"]).then_inc(wide_in, 16)
            sp.dma_start(lat, io["lat"]).then_inc(lat_in, 16)
            sp.dma_start(masks[:], io["c_masks"].bitcast(BF16)).then_inc(masks_in, 16)
            sp.dma_start(rope[:], io["c_rope"]).then_inc(rope_in, 16)
            for b in range(1, B):
                load_x(b)
            sp.dma_start(on_all[:], io["on_all"].broadcast_to((P, D + ER))).then_inc(late_in, 16)
            sp.dma_start(expert_ids[:], io["c_experts"]).then_inc(late_in, 16)
            for step in steps:
                kind, b = step[0], step[1] if len(step) > 1 else 0
                if kind == "KD":
                    wait_drained(sp, ("LK", b))
                    if b == 0:
                        sp.wait_ge(diag_zeroed, 2)
                        sp.wait_ge(tails_ready, 1)
                    else:
                        wait_full(sp, ("LS", b - 1, NLT - 1))
                    for h in range(H):
                        rows = slice(HD * h, HD * h + HD)
                        sp.dma_start(k_diag[rows, h, :], kT[rows, :]).then_inc(k_diag_in, 16)
                if kind == "MB":
                    side = step[2]
                    sp.wait_ge(split_ready, 2 * b + side + 1)
                    for hp in range(2):
                        for t0, nt, part in STORES[side]:
                            rows = slice(SLOT * hp, SLOT * hp + SLOT)
                            src = parts[rows, side, part:part + nt, :]
                            if side:
                                src = parts[rows, side, part:part + 1, :].broadcast_to((SLOT, nt, S))
                            sp.dma_start(parts_dram[b, side, hp, t0:t0 + nt].rearrange("t p n -> p t n"),
                                         src).then_inc(parts_out, 16)
                if kind == "ST" and b < 2:
                    sp.wait_ge(zeroed, b + 1)
                    for hp in range(2):
                        row = SLOT * hp + SHIFT_ROW
                        sp.dma_start(k_stack[b][row:row + 2, :, :],
                                     rows_dram[0:2, :].rearrange("o (a n) -> o a n", n=S)).then_inc(k_ones_in[b], 16)
                if kind == "ST":
                    sp.wait_ge(parts_out, 16 * 6 * 2 * (b + 1))
                    if b >= 2:
                        wait_full(sp, ("E", b - 2, H // 4 - 1, NT - 1, 0))
                    for side in range(2):
                        for hp in range(2):
                            src = parts_dram[b, side, hp].rearrange("t (d a) n -> (t d) a n", d=HD)
                            rows = slice(SLOT * hp, SLOT * hp + SHIFT_ROW)
                            dst = q_stack[b % 2][rows, :, hp, :] if side else k_stack[b % 2][rows, :, :]
                            sp.dma_start(dst, src).then_inc(stacks_in, 16)
                    for hp in range(2):
                        row = SLOT * hp + SHIFT_ROW
                        sp.dma_start(q_stack[b % 2][row:row + 2, :, hp, :],
                                     rows_dram[2:4, :].rearrange("o (a n) -> o a n", n=S)).then_inc(stacks_in, 16)
                if kind == "SHIFT":
                    _, b, g = step
                    n = b * (H // 4) + g
                    wait_drained(sp, step)
                    sp.dma_start(shift_dram[b, g].rearrange("r p n -> p r n"), shift[:]).then_inc(shift_out, 16)
                    sp.wait_ge(shift_out, 16 * (n + 1))
                    for hp in range(2):
                        row = SLOT * hp + SHIFT_ROW
                        src = shift_dram[b, g].rearrange("r (e a i) n -> e r a (i n)", e=2, i=NT)[hp]
                        sp.dma_start(q_stack[b % 2][row:row + 2, 2 * g:2 * g + 2, hp, :], src).then_inc(shift_in[g], 16)
                if kind == "WX":
                    wait_full(sp, ("LS", B - 1, NLT - 1))
                    for n, name in enumerate(("Wg", "Wu", "Wd")):
                        sp.dma_start(w_exp[:, 0, n, :], io[name + "_s"]).then_inc(experts_in, 16)
                        sp.dma_start(w_exp[:, 1:, n, :], io[name + "_r"].rearrange("e p i -> p e i")).then_inc(experts_in, 16)
                if kind == "DOWN" and step[2] == NE - 1:
                    sp.wait_ge(added, down_no[step])
                    sp.dma_start(out.rearrange("b (i p) d -> p b i d", p=P)[:, b],
                                 x[:, b * NT:(b + 1) * NT, :]).then_inc(out_done, 16)
            sp.wait_ge(out_done, 16 * B)

        @block.gpsimd
        def _(pool):
            own = [0]

            def link(ins):
                own[0] += 1
                ins.then_inc(g_step, 1)
                pool.wait_ge(g_step, own[0])

            def root(n, batches, rows=2):
                c = slice(batches[0] * NT, (batches[-1] + 1) * NT)
                pool.wait_ge(sqrt_in, n)
                nc.gpsimd.tensor_tensor(nrm[:, 6:6 + rows, c], nrm[:, 4:4 + rows, c], half[:, 0:rows, c],
                                        ALU.pow).then_inc(sqrt_out, 1)
                pool.wait_ge(sqrt_out, n)

            link(nc.gpsimd.memset(half[:], 0.5))
            link(nc.gpsimd.memset(k_diag[:, ACT_CLEARS:, :], 0.0))
            pool.sem_inc(diag_zeroed, 1)
            root(1, range(1))
            nc.gpsimd.memset(pT_loc[:], 0.0).then_inc(pT_cleared, 1)
            pool.wait_ge(pT_cleared, 1)

            def clear(i):
                nc.gpsimd.memset(k_stack[i][:].bitcast(F32), 0.0)
                nc.gpsimd.memset(q_stack[i][:].bitcast(F32), 0.0).then_inc(zeroed, 1)
                pool.wait_ge(zeroed, i + 1)

            clear(0)
            for step in steps:
                if step == ("STATS", 0):
                    root(2, range(1, B))
                if step[0] == "LN":
                    b = step[1]
                    tb = slice(b * NT, (b + 1) * NT)
                    pool.wait_ge(xn_ready, b + 1)
                    if b:
                        link(nc.gpsimd.tensor_tensor(xr[:, tb, :], xn[:, tb, :],
                                                     nrm[:, 3, tb].unsqueeze(2).broadcast_to((P, NT, D)), ALU.mult))
                        pool.sem_inc(xr_ready, 1)
                    pool.wait_ge(late_in, 16 * 2)
                    link(nc.gpsimd.tensor_tensor(x[:, tb, :], x[:, tb, :],
                                                 bo_all.unsqueeze(1).broadcast_to((P, NT, D)), ALU.add))
                    pool.sem_inc(bias_added, 1)
                if step[0] == "R2":
                    b = step[1]
                    tb = slice(b * NT, (b + 1) * NT)
                    root(b + 3, [b], 1)
                    wait_drained(pool, ("X1", b))
                    wait_drained(pool, ("LW", b))
                    link(nc.gpsimd.tensor_tensor(x[:, tb, :], x[:, tb, :], x1[:, tb, :], ALU.add))
                    pool.sem_inc(summed, 1)
                if step == ("MB", 1, 0):
                    clear(1)
                if step[0] == "MB" and step[1] == 0:
                    side = step[2]
                    pool.wait_ge(rounded, 2 * side + 1)
                    nc.gpsimd.tensor_tensor(rest[:], rot[:, side, :], parts[:, side, 0, :],
                                            ALU.subtract).then_inc(rest_ready, 1)
                    pool.wait_ge(rounded, 2 * side + 2)
                    pool.wait_ge(rest_ready, side + 1)
                    nc.gpsimd.tensor_tensor(parts[:, side, 2, :], rest[:], parts[:, side, 1, :],
                                            ALU.subtract).then_inc(split_ready, 1)
                    pool.wait_ge(split_ready, side + 1)
                if step[0] == "MB" and step[1] > 0:
                    _, b, side = step
                    n = 2 * b + side + 1
                    pool.wait_ge(rot_ready, n)
                    pool.wait_ge(split_ready, n - 1)
                    if side == 0:
                        pool.wait_ge(parts_out, 16 * 6 * 2 * b)
                    whole = rot[:, side, :]
                    hi, mid, lo = (parts[:, side, t, :] for t in range(3))
                    link(nc.gpsimd.tensor_copy(hi, whole))
                    link(nc.gpsimd.tensor_tensor(rest[:], whole, hi, ALU.subtract))
                    link(nc.gpsimd.tensor_copy(mid, rest[:]))
                    nc.gpsimd.tensor_tensor(lo, rest[:], mid, ALU.subtract).then_inc(split_ready, 1)
                    pool.wait_ge(split_ready, n)

        @block.scalar
        def _(act):
            nc.scalar.memzero(k_diag[:, 0:ACT_CLEARS, :]).then_inc(diag_zeroed, 1)
            act.wait_ge(wide_in, 16)

            def drain(use, dst, src, bias=None, scale=None):
                wait_full(act, use)
                if bias is None and scale is None:
                    ins = nc.scalar.copy(dst, src)
                elif bias is None:
                    ins = nc.scalar.activation(dst, src, ACT.Copy, scale=scale)
                else:
                    ins = nc.scalar.activation(dst, src, ACT.Identity, bias=bias)
                drained_by(ins, use)

            for step in steps:
                kind, b = step[0], step[1] if len(step) > 1 else 0
                bank = bank_of(step) if step in where else None
                if kind == "XT":
                    dst = xrT[:, b, :] if step[2] else xnT[:, b % 2, 0:S]
                    drain(step, dst, bank[:], scale=cols[:, 3:4] if step[2] else None)
                elif kind == "LQ":
                    if b >= 2:
                        wait_full(act, ("LS", b - 2, NLT - 1))
                    drain(step, qT[:, b % 2, 0:S], bank[:], bias=cols[:, 0:1])
                elif kind == "LK":
                    if b:
                        act.wait_ge(k_diag_in, 16 * H * b)
                    drain(step, kT[:, 0:S], bank[:], bias=cols[:, 1:2])
                elif kind == "MV":
                    if b >= 2:
                        act.wait_ge(pv_done, PV_PER_B * (b - 1))
                    if b < 2:
                        act.wait_ge(ones_set, 3)
                    drain(step, v_mla[:, b % 2, :, :, 0:HD], bank[:].rearrange("p (i h d) -> p i h d", i=NT, h=H))
                elif kind == "MB" and b == 0:
                    side = step[2]
                    act.wait_ge(rot_ready, side + 1)
                    nc.scalar.copy(parts[:, side, 0, :], rot[:, side, :]).then_inc(rounded, 1)
                    act.wait_ge(rest_ready, side + 1)
                    nc.scalar.copy(parts[:, side, 1, :], rest[:]).then_inc(rounded, 1)
                elif kind == "YT":
                    drain(step, yT_mla, bank[:])
                elif kind == "LV":
                    t = NLT * b + step[2]
                    if t < 2:
                        act.wait_ge(ones_set, 3)
                    else:
                        wait_full(act, ("LO", (t - 2) // NLT, (t - 2) % NLT))
                    np_ = PAIR * len(LTILES[step[2]])
                    drain(step, v_loc[0:np_, t % 2, :, 0:HD], bank[0:np_, 0:D].rearrange("p (h d) -> p h d", h=H))
                elif kind == "LR":
                    t = NLT * b + step[2]
                    act.wait_ge(loc_turned, t + 1)
                    act.wait_ge(pT_cleared, 1)
                    if t:
                        wait_full(act, ("LO", (t - 1) // NLT, (t - 1) % NLT))
                    for j in range(len(LTILES[step[2]])):
                        rows = slice(PAIR * j, PAIR * j + PAIR)
                        last = nc.scalar.activation(pT_loc[rows, :, rows],
                                                    sT_loc[rows, t % 2, :].rearrange("p (h k) -> p h k", h=H),
                                                    ACT.Exp, scale=SCALE)
                    last.then_inc(loc_exp, 1)
                elif kind == "LO":
                    drain(step, oT_loc[:], bank[:])
                elif kind == "LT" and step[2] < LOCAL_TILES:
                    if b and step[2] == 0:
                        wait_full(act, ("LW", b - 1))
                    drain(step, attnT[:, step[2] * P:(step[2] + 1) * P], bank[:, 0:P], bias=cols[:, 2:3])
                elif kind == "X2T":
                    drain(step, x2T[:, b, :], bank[:], scale=cols[:, 4:5])
                elif kind == "E":
                    _, b, g, j, u = step
                    n, w = pv_no[("PV", b, g, j)], S - j * P
                    heads = exp_units(g, j)[u]
                    if n > P_RING and u == 0:
                        act.wait_ge(pv_done, n - P_RING)
                    wait_full(act, step)
                    src = bank[:, 0:w * len(heads)].rearrange("p (h q) -> p h q", q=w)
                    m = heads[0] - 4 * g
                    drained_by(nc.scalar.activation(p_mla[:, n % P_RING, m:m + len(heads), j * P:], src,
                                                    ACT.Exp, scale=SCALE), step)
                elif kind == "PV" and step[3] == NT - 1:
                    _, b, g, _ = step
                    act.wait_ge(pv_done, pv_no[step])
                    if b and g == 0:
                        wait_full(act, ("X1", b - 1))
                    nc.scalar.copy(oT_mla[:, g, :], bank_c[:]).then_inc(c_drained, 1)
                elif kind == "ROUTE":
                    act.wait_ge(logits_ready, b + 1)
                    nc.scalar.activation(rt[:, 1, :, 0:ER], rt[:, 0, :, 0:ER], ACT.Exp, scale=-1.0).then_inc(logits_exp, 1)
                elif kind == "GU":
                    n = gu_no[step]
                    wait_full(act, step + (0,))
                    if n > 2:
                        act.wait_ge(hid_ready, n - 2)
                    nc.scalar.activation(gate[n % 2], bank_of(step + (0,))[:], ACT.Tanh, scale=0.5).then_inc(gate_ready, 1)

        @block.vector
        def _(dve):
            own = [0]

            def link(ins):
                own[0] += 1
                ins.then_inc(v_step, 1)
                dve.wait_ge(v_step, own[0])

            def begin_statistics(batches):
                ts = range(batches[0] * NT, (batches[-1] + 1) * NT)
                c = slice(ts[0], ts[-1] + 1)
                for t in ts:
                    if t % NT == 0:
                        dve.wait_ge(x_in[t // NT], 16)
                    last = nc.vector.bn_stats(stats[:, t, :], x[:, t, :])
                link(last)
                for t in ts:
                    last = nc.vector.bn_aggr(mv[:, t, :], stats[:, t, :])
                link(last)
                link(nc.vector.tensor_scalar(nrm[:, 4, c], mv[:, c, 1], LN_EPS, None, ALU.add))
                link(nc.vector.reciprocal(nrm[:, 2, c], nrm[:, 4, c]))
                nc.vector.tensor_tensor(nrm[:, 5, c], mv[:, c, 1], nrm[:, 2, c], ALU.mult).then_inc(sqrt_in, 1)

            def end_statistics(batches, n):
                c = slice(batches[0] * NT, (batches[-1] + 1) * NT)
                dve.wait_ge(sqrt_out, n)
                link(nc.vector.reciprocal(nrm[:, 2, c], nrm[:, 6, c]))
                link(nc.vector.tensor_scalar(nrm[:, 1, c], nrm[:, 7, c], RMS_EPS, None, ALU.add))
                link(nc.vector.reciprocal(nrm[:, 3, c], nrm[:, 1, c]))

            link(nc.vector.memset(nrm[:, 4:6, :], 1.0))
            begin_statistics(range(1))
            for bank in banks["M"]:
                nc.vector.memset(bank[:], 0.0)
            nc.vector.memset(bank_c[:], 0.0)
            nc.vector.memset(xnT[:, :, S:], 0.0).then_inc(set_up, 1)
            end_statistics(range(1), 1)

            def scratch_read(step):
                before = [s[0] for s in steps[:steps.index(step)]]
                for done, n in ((rot_ready, before.count("MB")), (loc_turned, before.count("LS"))):
                    if n:
                        dve.wait_ge(done, n)

            def outputs(step, dst, np_, den):
                o = bank_of(step)[0:np_, :].rearrange("p (h r) -> p h r", h=H)
                wait_full(dve, step)
                kind, b, i = step
                if i or b:
                    last = ((NLT if kind == "LY" else NT) - 1) if not i else i - 1
                    wait_drained(dve, (kind, b if i else b - 1, last))
                link(nc.vector.reciprocal(den[0:np_, :], o[:, :, HD]))
                drained_by(nc.vector.tensor_tensor(dst.rearrange("p (h d) -> p h d", h=H), o[:, :, 0:HD],
                                                   den[0:np_, :].unsqueeze(2).broadcast_to((np_, H, HD)), ALU.mult), step)

            for step in steps:
                kind, b = step[0], step[1] if len(step) > 1 else 0
                bank = bank_of(step) if step in where else None
                tb = slice(b * NT, (b + 1) * NT)
                if step == ("LK", 0):
                    dve.wait_ge(wide_in, 16)
                    nc.vector.tensor_scalar(kT[:, S:], xnT[:, 0, S:], cols[:, 1:2], None, ALU.add)
                    for n in range(2):
                        last = nc.vector.tensor_scalar(qT[:, n, S:], xnT[:, 0, S:], cols[:, 0:1], None, ALU.add)
                    last.then_inc(tails_ready, 1)
                    nc.vector.memset(attnT[:, S:], 0.0).then_inc(ones_set, 1)
                    nc.vector.memset(v_loc[:, :, :, HD:], 1.0).then_inc(ones_set, 1)
                    nc.vector.memset(v_mla[:, :, :, :, HD:], 1.0).then_inc(ones_set, 1)
                elif step == ("STATS", 0):
                    begin_statistics(range(1, B))
                elif step == ("STATS", 1):
                    end_statistics(range(1, B), 2)
                elif kind == "WF":
                    wait_full(dve, step)
                    ku, qu, rq = (bank[:, 64 * n:64 * n + 64].rearrange("p (a e d) -> p e d a", e=2, d=HH) for n in range(3))
                    rk = w_ropek.rearrange("p (a e) d -> p e d a", e=2)
                    part = HH // 2
                    nc.vector.memset(w_mla[:, :, 1, :, 0:HH, :], 0.0)
                    for e in range(2):
                        for side, plain, turn in ((0, ku, rk), (1, qu, rq)):
                            nc.vector.tensor_copy(w_mla[:, side, 0, e, 0:HH], plain[:, e])
                            nc.vector.tensor_copy(w_mla[:, side, 0, e, HH:], turn[:, e])
                            nc.vector.tensor_copy(w_mla[:, side, 1, e, HH:HH + part], turn[:, e, part:])
                            nc.vector.tensor_copy(w_mla[:, side, 1, e, HH + part:], turn[:, e, 0:part])
                    drained_by(nc.vector.tensor_copy(w_mla_v[:], bank[:, 192:192 + D]), step)
                elif kind == "LN":
                    for t in range(b * NT, b * NT + NT):
                        last = nc.vector.tensor_scalar(xn[:, t, :], x[:, t, :], mv[:, t, 0:1], nrm[:, 2, t:t + 1],
                                                       ALU.subtract, ALU.mult)
                    last.then_inc(xn_ready, 1)
                    if b == 0:
                        dve.wait_ge(xn_ready, 1)
                        for t in range(NT):
                            last = nc.vector.tensor_scalar(xr[:, t, :], xn[:, t, :], nrm[:, 3, t:t + 1], None, ALU.mult)
                        last.then_inc(xr_ready, 1)
                elif kind in ("MA", "MB"):
                    side, which = step[2], int(kind == "MB")
                    if b and which == 0:
                        dve.wait_ge(split_ready, 2 * (b - 1) + side + 1)
                    if which:
                        scratch_read(step)
                    dve.wait_ge(rope_in, 16)
                    wait_full(dve, step)
                    dst = turned[:] if which else rot[:, side, :]
                    drained_by(nc.vector.tensor_tensor(dst, bank[:], rope[:, which, :], ALU.mult), step)
                    if which:
                        wait_drained(dve, step)
                        nc.vector.tensor_tensor(rot[:, side, :], rot[:, side, :], turned[:], ALU.add).then_inc(rot_ready, 1)
                elif kind == "S":
                    i, heads = UNITS[step[2]]
                    w = (i + 1) * P
                    wait_full(dve, step)
                    src = bank[:, 0:w * len(heads)].rearrange("p (h k) -> p h k", k=w)
                    g, a0, e0 = heads[0] // 4, heads[0] % 4 // 2, heads[0] % 2
                    if i >= 2:
                        dst = neg_max[:, g, e0, a0, i:i + 1]
                        n = single.index(step)
                        if n:
                            wait_drained(dve, single[n - 1])
                        drained_by(nc.vector.tensor_tensor_reduce(differences[:, 0:w], masked16[:, S - w:],
                                                                  bank[:, 0:w], -1.0, -NEG, ALU.add, ALU.min, dst), step)
                    else:
                        dst = neg_max[:, g, :, a0:a0 + len(heads) // 2, i].rearrange("p e a -> p a e")
                        src = src.rearrange("p (a e) k -> p a e k", e=2)
                        drained_by(nc.vector.tensor_reduce(dst, src, AX.X, ALU.max, negate=True), step)
                elif kind == "SHIFT":
                    n = b * (H // 4) + step[2]
                    wait_full(dve, step)
                    if n:
                        dve.wait_ge(shift_out, 16 * n)
                    link(nc.vector.tensor_copy(shift[:, 0, :], bank[0:4 * NT, 0:P]))
                    drained_by(nc.vector.tensor_tensor(shift[:, 1, :], bank[0:4 * NT, 0:P], shift[:, 0, :],
                                                       ALU.subtract), step)
                elif kind == "LS":
                    t = NLT * b + step[2]
                    np_ = PAIR * len(LTILES[step[2]])
                    sc = bank[0:np_, :].rearrange("p (h k) -> p h k", h=H)
                    wait_full(dve, step)
                    scratch_read(step)
                    link(nc.vector.tensor_reduce(row_max[0:np_, :], sc, AX.X, ALU.max))
                    drained_by(nc.vector.tensor_tensor(s_loc[0:np_, :].rearrange("p (h k) -> p h k", h=H), sc,
                                                       row_max[0:np_, :].unsqueeze(2).broadcast_to((np_, H, PAIR)),
                                                       ALU.subtract), step)
                    wait_drained(dve, step)
                    if t >= 2:
                        dve.wait_ge(loc_exp, t - 1)
                    nc.vector.transpose(sT_loc[0:np_, t % 2, :], s_loc[0:np_, :]).then_inc(loc_turned, 1)
                elif kind == "LY":
                    np_ = PAIR * len(LTILES[step[2]])
                    outputs(step, y_loc[0:np_, :], np_, rden)
                elif kind == "LT" and step[2] >= LOCAL_TILES:
                    wait_full(dve, step)
                    if step[2] == LOCAL_TILES:
                        for l in range(LOCAL_TILES):
                            wait_drained(dve, ("LT", b, l))
                    for g0, ng, first, stp in runs(LTILES[step[2]]):
                        dst = attnT[:, tokens(first, stp, PAIR * ng)]
                        last = nc.vector.scalar_tensor_tensor(out=dst, in0=bank[:, g0 * PAIR:(g0 + ng) * PAIR],
                                                              scalar=cols[:, 2:3], in1=dst, op0=ALU.add, op1=ALU.add)
                    drained_by(last, step)
                elif kind == "LW":
                    dve.wait_ge(bias_added, b + 1)
                    wait_full(dve, step)
                    drained_by(nc.vector.tensor_tensor(x[:, tb, :], bank[:].rearrange("p (i d) -> p i d", i=NT),
                                                       x[:, tb, :], ALU.add), step)
                elif kind == "Y":
                    outputs(step, y_mla[:, step[2], :], P, rden_mla)
                elif kind == "X1":
                    wait_full(dve, step)
                    drained_by(nc.vector.tensor_tensor(x1[:, tb, :], bank[:].rearrange("p (i d) -> p i d", i=NT),
                                                       xn[:, tb, :], ALU.add), step)
                elif kind == "R2":
                    wait_drained(dve, ("X1", b))
                    for t in range(b * NT, b * NT + NT):
                        last = nc.vector.tensor_tensor_reduce(xn[:, t, :], x1[:, t, :], x1[:, t, :], 1.0 / D, 0.0,
                                                              ALU.mult, ALU.add, nrm[:, 4, t:t + 1])
                    last.then_inc(sqrt_in, 1)
                elif kind == "R3":
                    dve.wait_ge(sqrt_out, b + 3)
                    link(nc.vector.tensor_scalar(nrm[:, 1, tb], nrm[:, 6, tb], RMS_EPS, None, ALU.add))
                    link(nc.vector.reciprocal(nrm[:, 2, tb], nrm[:, 1, tb]))
                    for t in range(b * NT, b * NT + NT):
                        last = nc.vector.tensor_scalar(xn[:, t, :], x1[:, t, :], nrm[:, 2, t:t + 1], None, ALU.mult)
                    last.then_inc(x2_ready, 1)
                elif kind == "ROUTE":
                    wait_full(dve, step)
                    drained_by(nc.vector.tensor_tensor(rt[:, 0, :, 0:ER],
                                                       bank[:, 0:NT * ER].rearrange("p (t e) -> p t e", e=ER),
                                                       router_bias.unsqueeze(1).broadcast_to((P, NT, ER)), ALU.add), step)
                    wait_drained(dve, step)
                    nc.vector.memset(rt[:, 3, :, ER:], -1.0).then_inc(logits_ready, 1)
                elif kind == "PICK":
                    dve.wait_ge(logits_exp, b + 1)
                    link(nc.vector.tensor_scalar(rt[:, 1, :, 0:ER], rt[:, 1, :, 0:ER], 1.0, None, ALU.add))
                    link(nc.vector.reciprocal(rt[:, 3, :, 0:ER], rt[:, 1, :, 0:ER]))
                    for t in range(NT):
                        last = nc.vector.max(rt[:, 2, t, :], rt[:, 3, t, :])
                    link(last)
                    for t in range(NT):
                        last = nc.vector.max_index(rt_idx[:, t, :], rt[:, 2, t, :], rt[:, 3, t, :])
                    link(last)
                    link(nc.vector.tensor_copy(rt[:, 0, :, :], rt_idx[:]))
                    link(nc.vector.tensor_tensor(rt_sum[:, 0, :], rt[:, 2, :, 0], rt[:, 2, :, 1], ALU.add))
                    link(nc.vector.reciprocal(rt_sum[:, 1, :], rt_sum[:, 0, :]))
                    link(nc.vector.tensor_scalar(rt_sum[:, 1, :], rt_sum[:, 1, :], 0.5, None, ALU.mult))
                    link(nc.vector.tensor_tensor(rt[:, 2, :, 0:2], rt[:, 2, :, 0:2],
                                                 rt_sum[:, 1, :].unsqueeze(2).broadcast_to((P, NT, 2)), ALU.mult))
                    for n in range(2):
                        link(nc.vector.tensor_tensor(rt[:, 4 + n, :, :], rt[:, 0, :, n:n + 1].broadcast_to((P, NT, 8)),
                                                     expert_ids[:].unsqueeze(1).broadcast_to((P, NT, 8)), ALU.is_equal))
                        link(nc.vector.tensor_tensor(rt[:, 4 + n, :, :], rt[:, 4 + n, :, :],
                                                     rt[:, 2, :, n:n + 1].broadcast_to((P, NT, 8)), ALU.mult))
                    link(nc.vector.tensor_tensor(expert_w[:, tb, :], rt[:, 4, :, :], rt[:, 5, :, :], ALU.add))
                elif kind == "GU":
                    n = gu_no[step]
                    dve.wait_ge(gate_ready, n)
                    if n > 2:
                        wait_full(dve, downs[n - 3])
                    drained_by(nc.vector.scalar_tensor_tensor(out=hid[n % 2], in0=gate[n % 2], scalar=1.0,
                                                              in1=bank_of(step + (0,))[:], op0=ALU.add, op1=ALU.mult),
                               step + (0,))
                    wait_drained(dve, step + (0,))
                    wait_full(dve, step + (1,))
                    ins = nc.vector.tensor_tensor(hid[n % 2], bank_of(step + (1,))[:], hid[n % 2], ALU.mult)
                    drained_by(ins, step + (1,))
                    wait_drained(dve, step + (1,))
                    dve.sem_inc(hid_ready, 1)
                elif kind == "DOWN":
                    _, c, e = step
                    if e == 0:
                        dve.wait_ge(summed, c + 1)
                    wait_full(dve, step)
                    down = bank[:].rearrange("p (i d) -> p i d", i=NT)
                    if down_no[step] > 1:
                        dve.wait_ge(added, down_no[step] - 1)
                    for i in range(NT):
                        t = c * NT + i
                        weight = 0.5 if e == 0 else expert_w[:, t, e - 1:e]
                        ins = nc.vector.scalar_tensor_tensor(out=x[:, t, :], in0=down[:, i, :], scalar=weight,
                                                             in1=x[:, t, :], op0=ALU.mult, op1=ALU.add)
                    drained_by(ins, step)
                    wait_drained(dve, step)
                    dve.sem_inc(added, 1)

        @block.tensor
        def _(pe):
            pe.wait_ge(set_up, 1)
            pe.wait_ge(eye_in, 16)
            for _ in range(6):
                nc.tensor.matmul(bank_c[:, 0:P], eye[:], eye[:], start=True, stop=True)
            for step in steps:
                kind, b = step[0], step[1] if len(step) > 1 else 0
                if step in where and kind != "SHIFT":
                    wait_free(pe, step)
                    bank = bank_of(step)
                if kind == "WF":
                    pe.wait_ge(lat_in, 16)
                    for down, c0, c1 in ((0, 0, 64), (1, 64, 128), (1, 128, 192), (0, 192, 192 + D)):
                        last = nc.tensor.matmul(bank[:, c0:c1], w_down_lat[:, down, :], w_up_lat[:, c0:c1],
                                                start=True, stop=True)
                    full_by(last, step)
                elif kind in ("XT", "X2T"):
                    second = kind == "X2T"
                    if second:
                        pe.wait_ge(x2_ready, b + 1)
                    else:
                        pe.wait_ge(xr_ready if step[2] else xn_ready, b + 1)
                    src = xr if not second and step[2] else xn
                    for i in range(NT):
                        last = nc.tensor.transpose(bank[:, i * P:(i + 1) * P], src[:, b * NT + i, :], eye[:])
                    full_by(last, step)
                elif kind in ("LQ", "LK"):
                    pe.wait_ge(wide_in, 16)
                    wait_drained(pe, ("XT", b, 0))
                    full_by(nc.tensor.matmul(bank[:], w_attn[:, int(kind == "LK"), :], xnT[:, b % 2, 0:S], start=True,
                                             stop=True), step)
                elif kind in ("MA", "MB"):
                    wait_drained(pe, ("WF",))
                    wait_drained(pe, ("XT", b, 1))
                    full_by(nc.tensor.matmul(bank[:], w_mla[:, step[2], int(kind == "MB")].rearrange("p e d a -> p (e d a)"), xrT[:, b, :], start=True,
                                             stop=True), step)
                elif kind == "MV":
                    for i in range(NT):
                        last = nc.tensor.matmul(bank[:, i * D:(i + 1) * D], xrT[:, b, i * P:(i + 1) * P], w_mla_v[:],
                                                start=True, stop=True)
                    full_by(last, step)
                elif kind == "S":
                    i, heads = UNITS[step[2]]
                    w = (i + 1) * P
                    if step[2] == 0:
                        pe.wait_ge(k_ones_in[b % 2], 16 * 2)
                        pe.wait_ge(stacks_in, STACK_IN * (b + 1))
                    for n, h in enumerate(heads):
                        last = nc.tensor.matmul(bank[:, n * w:(n + 1) * w],
                                                q_stack[b % 2][:, h // 2, h % 2, i * P:(i + 1) * P],
                                                k_stack[b % 2][:, h // 2, 0:w], start=True, stop=i >= 2,
                                                skip_group_check=True)
                        if i < 2:
                            last = nc.tensor.matmul(bank[:, (n + 1) * w - P:(n + 1) * w], eye16, causal16,
                                                    start=False, stop=True, skip_group_check=True)
                    full_by(last, step)
                elif kind == "SHIFT":
                    g = step[2]
                    wait_drained(pe, ("S", b, PER_GROUP * (g + 1) - 1))
                    wait_free(pe, step)
                    full_by(nc.tensor.transpose(bank_of(step)[0:4 * NT, 0:P],
                                                neg_max[:, g].rearrange("p e a i -> p (e a i)"), eye[:]), step)
                elif kind == "E":
                    _, b, g, j, u = step
                    w = S - j * P
                    if (j, u) == (0, 0):
                        pe.wait_ge(shift_in[g], 32 * (b + 1))
                    for m, h in enumerate(exp_units(g, j)[u]):
                        nc.tensor.matmul(bank[:, m * w:(m + 1) * w], k_stack[b % 2][:, h // 2, j * P:(j + 1) * P],
                                         q_stack[b % 2][:, h // 2, h % 2, j * P:], start=True, stop=False,
                                         skip_group_check=True)
                        last = nc.tensor.matmul(bank[:, m * w:m * w + P], eye16, causalT16,
                                                start=False, stop=True, skip_group_check=True)
                    full_by(last, step)
                elif kind == "PV":
                    _, b, g, j = step
                    n = pv_no[step]
                    wait_drained(pe, ("E", b, g, j, len(exp_units(g, j)) - 1))
                    wait_drained(pe, ("MV", b))
                    if j == 0 and n > 1:
                        pe.wait_ge(c_drained, (n - 1) // NT)
                    for m in range(4):
                        last = nc.tensor.matmul(bank_c[32 * m:32 * m + HD + 1, j * P:], v_mla[:, b % 2, j, 4 * g + m, :],
                                                p_mla[:, n % P_RING, m, j * P:], start=(j == 0), stop=(j == NT - 1),
                                                skip_group_check=True)
                    last.then_inc(pv_done, 1)
                elif kind == "Y":
                    if step[2] == 0:
                        pe.wait_ge(c_drained, (b + 1) * (H // 4))
                    for g in range(4):
                        last = nc.tensor.transpose(bank[:, g * P:(g + 1) * P], oT_mla[:, g, step[2] * P:(step[2] + 1) * P],
                                                   eye[:])
                    full_by(last, step)
                elif kind == "YT":
                    wait_drained(pe, ("Y", b, NT - 1))
                    for i in range(NT):
                        last = nc.tensor.transpose(bank[:, i * P:(i + 1) * P], y_mla[:, i, :], eye[:])
                    full_by(last, step)
                elif kind == "X1":
                    wait_drained(pe, ("YT", b))
                    for i in range(NT):
                        last = nc.tensor.matmul(bank[:, i * D:(i + 1) * D], yT_mla[:, i * P:(i + 1) * P], w_mla_o,
                                                start=True, stop=True)
                    full_by(last, step)
                elif kind == "LV":
                    for j, (_, first, stp) in enumerate(LTILES[step[2]]):
                        last = nc.tensor.matmul(bank[PAIR * j:PAIR * j + PAIR, 0:D], xnT[:, b % 2, tokens(first, stp)],
                                                w_attn[:, 2, :], start=True, stop=True, skip_group_check=True)
                    full_by(last, step)
                elif kind == "LS":
                    if step[2] == 0:
                        pe.wait_ge(k_diag_in, 16 * H * (b + 1))
                        wait_drained(pe, ("LQ", b))
                        if b == 0:
                            pe.wait_ge(masks_in, 16)
                            pe.wait_ge(tails_ready, 1)
                    np_ = PAIR * len(LTILES[step[2]])
                    nc.tensor.matmul(bank[0:np_, :], eye16[:, 0:np_], pair16, start=True, stop=False, skip_group_check=True)
                    for j, (_, first, stp) in enumerate(LTILES[step[2]]):
                        last = nc.tensor.matmul(bank[PAIR * j:PAIR * j + PAIR, :], qT[:, b % 2, tokens(first, stp)],
                                                k_diag[:, :, tokens(first, stp)], start=False, stop=True,
                                                skip_group_check=True)
                    full_by(last, step)
                elif kind == "LO":
                    t = NLT * b + step[2]
                    np_ = PAIR * len(LTILES[step[2]])
                    pe.wait_ge(loc_exp, t + 1)
                    wait_drained(pe, ("LV", b, step[2]))
                    for h in range(H):
                        m, c = h % 4, h // 4 * P
                        last = nc.tensor.matmul(bank[32 * m:32 * m + HD + 1, c:c + np_], v_loc[0:np_, t % 2, h, :],
                                                pT_loc[0:np_, h, 0:np_], start=True, stop=True, skip_group_check=True)
                    full_by(last, step)
                elif kind == "LY":
                    np_ = PAIR * len(LTILES[step[2]])
                    wait_drained(pe, ("LO", b, step[2]))
                    for g in range(4):
                        last = nc.tensor.transpose(bank[0:np_, g * P:(g + 1) * P], oT_loc[:, g * P:g * P + np_], eye[:])
                    full_by(last, step)
                elif kind == "LT":
                    np_ = PAIR * len(LTILES[step[2]])
                    wait_drained(pe, ("LY", b, step[2]))
                    full_by(nc.tensor.transpose(bank[:, 0:np_], y_loc[0:np_, :], eye[0:np_, 0:np_]), step)
                elif kind == "LW":
                    wait_drained(pe, ("LT", b, NLT - 1))
                    for i in range(NT):
                        last = nc.tensor.matmul(bank[:, i * D:(i + 1) * D], attnT[:, i * P:(i + 1) * P], w_attn[:, 3, :],
                                                start=True, stop=True)
                    full_by(last, step)
                elif kind == "ROUTE":
                    wait_drained(pe, ("X2T", b))
                    for i in range(NT):
                        last = nc.tensor.matmul(bank[:, i * ER:(i + 1) * ER], x2T[:, b, i * P:(i + 1) * P],
                                                w_router, start=True, stop=True)
                    full_by(last, step)
                elif kind == "GU":
                    _, c, e = step
                    if e == 0:
                        wait_drained(pe, ("X2T", c))
                        pe.wait_ge(experts_in, 16 * 6)
                    for m in range(2):
                        use = step + (m,)
                        wait_free(pe, use)
                        full_by(nc.tensor.matmul(bank_of(use)[:], w_exp[:, e, m, :], x2T[:, c, :], start=True, stop=True), use)
                elif kind == "DOWN":
                    _, c, e = step
                    n = gu_no[("GU", c, e)]
                    pe.wait_ge(hid_ready, n)
                    for i in range(NT):
                        last = nc.tensor.matmul(bank[:, i * D:(i + 1) * D], hid[n % 2][:, i * P:(i + 1) * P],
                                                w_exp[:, e, 2, :], start=True, stop=True)
                    full_by(last, step)


_TURNED = ("Wq", "Wk", "Wv", "Wo", "W_kvd", "W_qd")
_NAMES = ["L0_attn_" + n for n in ("x", "Wq", "bq", "Wk", "bk", "Wv", "bv", "Wo", "bo")] + ["L0_ffn_" + n for n in (
    "w_ln1", "w_ln2", "W_kvd", "W_qd", "W_ku", "W_qu", "W_vu", "W_ropeq", "W_ropek", "W_o", "Wg_s", "Wu_s", "Wd_s",
    "Wg_r", "Wu_r", "Wd_r", "W_router", "routing_bias")]


def kernel(**inputs):
    import numpy as _np
    import concourse.bacc as _bacc
    from concourse import mybir as _mybir
    from concourse.bass_utils import run_bass_kernel_spmd as _run

    nc = _bacc.Bacc("TRN2", target_bir_lowering=False, num_devices=1)
    laid = {}
    for full in _NAMES:
        name = full.split("_", 2)[2]
        a = _np.asarray(inputs[full])
        laid[name] = _np.ascontiguousarray(a.T if name in _TURNED else a)
    laid["wide"] = _np.concatenate([laid.pop(n).reshape(P, -1) for n in WIDE], axis=1)
    laid["lat"] = _np.concatenate([laid.pop(n) for n in LATS], axis=1)
    laid["on_all"] = _np.concatenate([laid.pop(n) for n in ("bo", "routing_bias")])[None]
    laid.update(constants())
    arrays, io = {}, {}
    for name, a in laid.items():
        arrays[f"in_{name}"] = a
        io[name] = nc.dram_tensor(f"in_{name}", a.shape, _mybir.dt.from_np(a.dtype), kind="ExternalInput").ap()
    out = nc.dram_tensor("out_0", (B, S, D), _mybir.dt.float32, kind="ExternalOutput").ap()
    build(nc, io, out)
    r = _run(nc, [arrays], core_ids=[0])
    return r.results[0]["out_0"]
```
